# Optimizing a Trainium2 kernel written in Bass

```python
import numpy as np
import jax
import jax.numpy as jnp

def _softmax(x, axis=-1):
    return jax.nn.softmax(x, axis=axis)

def _gelu(x):
    return jax.nn.gelu(x, approximate=True)

def _silu(x):
    return jax.nn.silu(x)

def _sigmoid(x):
    return jax.nn.sigmoid(x)

def _layernorm(x, axis=-1, eps=1e-05):
    m = jnp.mean(x, axis=axis, keepdims=True)
    v = jnp.var(x, axis=axis, keepdims=True)
    return (x - m) / jnp.sqrt(v + eps)

def _scatter_add(tgt, idx, src, axis=0):
    return tgt.at[idx].add(src)

def _segment_sum(src, seg, n):
    return jax.ops.segment_sum(src, seg, n)
kernel_name = 'mk_macaron_d1_jaxref_r8_f6351e'

def setup_inputs(seed: int=0):
    np.random.seed(seed)
    _w = jnp.asarray

    def _L0_attn_setup():
        import jax, jax.numpy as jnp
        import numpy as np
        B_SZ, L, D_MODEL = (2, 128, 128)
        D_INNER, D_STATE, D_CONV = (256, 16, 4)
        EPS = 1e-06

        def _selective_scan(xc, delta, A, Bm, Cm, D_skip):
            dA = jnp.exp(delta[..., None] * A)
            dBx = (delta * xc)[..., None] * Bm[:, :, None, :]
            h0 = jnp.zeros((xc.shape[0], xc.shape[2], A.shape[1]), xc.dtype)

            def step(h, inp):
                dA_t, dBx_t, C_t = inp
                h = dA_t * h + dBx_t
                y_t = jnp.einsum('bds,bs->bd', h, C_t)
                return (h, y_t)
            _, ys = jax.lax.scan(step, h0, (dA.transpose(1, 0, 2, 3), dBx.transpose(1, 0, 2, 3), Cm.transpose(1, 0, 2)))
            y = ys.transpose(1, 0, 2)
            return y + D_skip * xc

        def _layernorm(r, alpha, beta):
            mean = jnp.mean(r, axis=-1, keepdims=True)
            diff = r - mean
            var_unb = jnp.sum(diff * diff, axis=-1, keepdims=True) / (r.shape[-1] - 1)
            std = jnp.sqrt(var_unb)
            return alpha * diff / (std + EPS) + beta
        key = jax.random.key(seed)
        ks = jax.random.split(key, 8)

        def n(k, shape, scale=0.02):
            return jax.random.normal(k, shape, jnp.float32) * scale
        return {'x': jax.random.normal(ks[0], (B_SZ, L, D_MODEL), jnp.float32), 'W_in': n(ks[1], (D_MODEL, 2 * D_INNER)), 'b_in': jnp.zeros((2 * D_INNER,), jnp.float32), 'conv_w': n(ks[2], (D_INNER, 1, D_CONV), 0.2), 'conv_b': jnp.zeros((D_INNER,), jnp.float32), 'W_xp': n(ks[3], (D_INNER, 2 * D_STATE)), 'b_xp': jnp.zeros((2 * D_STATE,), jnp.float32), 'W_dt': n(ks[4], (D_INNER, D_INNER)), 'b_dt': jnp.full((D_INNER,), -1.0, jnp.float32), 'A_log': jnp.log(jax.random.uniform(ks[5], (D_INNER, D_STATE), jnp.float32, 0.5, 1.5)), 'D_skip': jnp.ones((D_INNER,), jnp.float32), 'W_out': n(ks[6], (D_INNER, D_MODEL)), 'b_out': jnp.zeros((D_MODEL,), jnp.float32), 'alpha': jnp.ones((D_MODEL,), jnp.float32), 'beta': jnp.zeros((D_MODEL,), jnp.float32)}
    _L0_attn_in = _L0_attn_setup()

    def _L0_ffn_setup():
        import jax, jax.numpy as jnp
        import numpy as np
        B, T, C = (4, 256, 128)
        E = 8
        K = 2
        H = 176
        HS = 176 * 2
        key = jax.random.key(seed)
        k = jax.random.split(key, 8)
        s = 0.02
        return {'x': jax.random.normal(k[0], (B, T, C), jnp.float32), 'Wg': jax.random.normal(k[1], (C, E), jnp.float32) * s, 'W1': jax.random.normal(k[2], (E, C, H), jnp.float32) * s, 'W2': jax.random.normal(k[3], (E, C, H), jnp.float32) * s, 'W3': jax.random.normal(k[4], (E, H, C), jnp.float32) * s, 'Ws1': jax.random.normal(k[5], (C, HS), jnp.float32) * s, 'Ws2': jax.random.normal(k[6], (C, HS), jnp.float32) * s, 'Ws3': jax.random.normal(k[7], (HS, C), jnp.float32) * s}
    _L0_ffn_in = _L0_ffn_setup()
    _d = {'L0_attn_x': _L0_attn_in['x'], 'L0_attn_W_in': _L0_attn_in['W_in'], 'L0_attn_b_in': _L0_attn_in['b_in'], 'L0_attn_conv_w': _L0_attn_in['conv_w'], 'L0_attn_conv_b': _L0_attn_in['conv_b'], 'L0_attn_W_xp': _L0_attn_in['W_xp'], 'L0_attn_b_xp': _L0_attn_in['b_xp'], 'L0_attn_W_dt': _L0_attn_in['W_dt'], 'L0_attn_b_dt': _L0_attn_in['b_dt'], 'L0_attn_A_log': _L0_attn_in['A_log'], 'L0_attn_D_skip': _L0_attn_in['D_skip'], 'L0_attn_W_out': _L0_attn_in['W_out'], 'L0_attn_b_out': _L0_attn_in['b_out'], 'L0_attn_alpha': _L0_attn_in['alpha'], 'L0_attn_beta': _L0_attn_in['beta'], 'L0_ffn_Wg': _L0_ffn_in['Wg'], 'L0_ffn_W1': _L0_ffn_in['W1'], 'L0_ffn_W2': _L0_ffn_in['W2'], 'L0_ffn_W3': _L0_ffn_in['W3'], 'L0_ffn_Ws1': _L0_ffn_in['Ws1'], 'L0_ffn_Ws2': _L0_ffn_in['Ws2'], 'L0_ffn_Ws3': _L0_ffn_in['Ws3']}
    _x0 = _d['L0_attn_x']
    _d['L0_attn_x'] = jax.random.normal(jax.random.fold_in(jax.random.key(seed), 1), (32, 256, 128), dtype=_x0.dtype)
    del _x0
    return _d

def reference(L0_attn_x, L0_attn_W_in, L0_attn_b_in, L0_attn_conv_w, L0_attn_conv_b, L0_attn_W_xp, L0_attn_b_xp, L0_attn_W_dt, L0_attn_b_dt, L0_attn_A_log, L0_attn_D_skip, L0_attn_W_out, L0_attn_b_out, L0_attn_alpha, L0_attn_beta, L0_ffn_Wg, L0_ffn_W1, L0_ffn_W2, L0_ffn_W3, L0_ffn_Ws1, L0_ffn_Ws2, L0_ffn_Ws3):

    def _L0_attn_ref(x, W_in, b_in, conv_w, conv_b, W_xp, b_xp, W_dt, b_dt, A_log, D_skip, W_out, b_out, alpha, beta):
        import jax, jax.numpy as jnp
        import numpy as np
        B_SZ, L, D_MODEL = (2, 128, 128)
        D_INNER, D_STATE, D_CONV = (256, 16, 4)
        EPS = 1e-06

        def _selective_scan(xc, delta, A, Bm, Cm, D_skip):
            dA = jnp.exp(delta[..., None] * A)
            dBx = (delta * xc)[..., None] * Bm[:, :, None, :]
            h0 = jnp.zeros((xc.shape[0], xc.shape[2], A.shape[1]), xc.dtype)

            def step(h, inp):
                dA_t, dBx_t, C_t = inp
                h = dA_t * h + dBx_t
                y_t = jnp.einsum('bds,bs->bd', h, C_t)
                return (h, y_t)
            _, ys = jax.lax.scan(step, h0, (dA.transpose(1, 0, 2, 3), dBx.transpose(1, 0, 2, 3), Cm.transpose(1, 0, 2)))
            y = ys.transpose(1, 0, 2)
            return y + D_skip * xc

        def _layernorm(r, alpha, beta):
            mean = jnp.mean(r, axis=-1, keepdims=True)
            diff = r - mean
            var_unb = jnp.sum(diff * diff, axis=-1, keepdims=True) / (r.shape[-1] - 1)
            std = jnp.sqrt(var_unb)
            return alpha * diff / (std + EPS) + beta
        residual = x
        xz = x @ W_in + b_in
        x_in, z = jnp.split(xz, 2, axis=-1)
        xt = x_in.transpose(0, 2, 1)
        xt = jax.lax.conv_general_dilated(xt, conv_w, window_strides=(1,), padding=[(D_CONV - 1, 0)], feature_group_count=D_INNER, dimension_numbers=('NCH', 'OIH', 'NCH'))
        xt = xt + conv_b[None, :, None]
        x_conv = jax.nn.silu(xt.transpose(0, 2, 1))
        x_proj_out = x_conv @ W_xp + b_xp
        Bm, Cm = jnp.split(x_proj_out, 2, axis=-1)
        delta = jax.nn.softplus(x_conv @ W_dt + b_dt)
        A = -jnp.exp(A_log)
        y = _selective_scan(x_conv, delta, A, Bm, Cm, D_skip)
        y = y * jax.nn.silu(z)
        out = y @ W_out + b_out
        return _layernorm(residual + out, alpha, beta)

    def _L0_ffn_ref(x, Wg, W1, W2, W3, Ws1, Ws2, Ws3):
        import jax, jax.numpy as jnp
        import numpy as np
        B, T, C = (4, 256, 128)
        E = 8
        K = 2
        H = 176
        HS = 176 * 2
        b, t, c = x.shape
        xf = x.reshape(-1, c)
        n = xf.shape[0]
        router = xf @ Wg
        top_logits, idx = jax.lax.top_k(router, K)
        probs = jax.nn.softmax(top_logits.astype(jnp.float32), axis=-1).astype(x.dtype)
        w = jnp.zeros((n, E), x.dtype).at[jnp.arange(n)[:, None], idx].add(probs)
        h = jax.nn.silu(jnp.einsum('tc,ech->eth', xf, W1)) * jnp.einsum('tc,ech->eth', xf, W2)
        y = jnp.einsum('eth,ehc,te->tc', h, W3, w)
        y = y.reshape(b, t, c)
        hs = jax.nn.silu(xf @ Ws1) * (xf @ Ws2)
        y = y + (hs @ Ws3).reshape(b, t, c)
        return y
    x = L0_attn_x
    x = x + 0.5 * _L0_ffn_ref(_layernorm(x, axis=-1), L0_ffn_Wg, L0_ffn_W1, L0_ffn_W2, L0_ffn_W3, L0_ffn_Ws1, L0_ffn_Ws2, L0_ffn_Ws3)
    x = x + _L0_attn_ref(_layernorm(x, axis=-1), L0_attn_W_in, L0_attn_b_in, L0_attn_conv_w, L0_attn_conv_b, L0_attn_W_xp, L0_attn_b_xp, L0_attn_W_dt, L0_attn_b_dt, L0_attn_A_log, L0_attn_D_skip, L0_attn_W_out, L0_attn_b_out, L0_attn_alpha, L0_attn_beta)
    x = x + 0.5 * _L0_ffn_ref(_layernorm(x, axis=-1), L0_ffn_Wg, L0_ffn_W1, L0_ffn_W2, L0_ffn_W3, L0_ffn_Ws1, L0_ffn_Ws2, L0_ffn_Ws3)
    return x

_drawn_inputs = setup_inputs


def setup_inputs(seed=0):
    import zlib

    import numpy as np

    out = dict(_drawn_inputs(seed))
    spreads = {'L0_attn_b_in': (0.0, 0.8),
     'L0_attn_conv_b': (0.0, 0.8),
     'L0_attn_b_xp': (0.0, 0.8),
     'L0_attn_b_dt': (-1.0, 0.6),
     'L0_attn_D_skip': (1.0, 0.6),
     'L0_attn_b_out': (0.0, 0.1),
     'L0_attn_alpha': (1.0, 0.2),
     'L0_attn_beta': (0.0, 0.1)}
    factors = {'L0_attn_W_in': 8.0,
     'L0_attn_conv_w': 8.0,
     'L0_attn_W_xp': 8.0,
     'L0_attn_W_dt': 8.0,
     'L0_attn_A_log': 8.0,
     'L0_attn_W_out': 8.0,
     'L0_ffn_Wg': 8.0,
     'L0_ffn_W1': 8.0,
     'L0_ffn_W2': 8.0,
     'L0_ffn_W3': 8.0,
     'L0_ffn_Ws1': 7.898,
     'L0_ffn_Ws2': 7.872,
     'L0_ffn_Ws3': 7.883}
    for name, (base, spread) in spreads.items():
        noise = np.random.default_rng([zlib.crc32(name.encode()), seed]).standard_normal(out[name].shape)
        drawn = base * np.exp(spread * noise) if base else spread * noise
        out[name] = jnp.asarray(drawn.astype(out[name].dtype))
    for name, factor in factors.items():
        out[name] = (out[name] * factor).astype(out[name].dtype)
    return out
```

```python
import math
from contextlib import ExitStack

import numpy as np
import concourse.bass as bass
from concourse import mybir


def macaron_kernel(nc, x, W_in, b_in, conv_w, conv_b, W_xp, b_xp, W_dt, b_dt, A_log, D_skip, W_out, b_out,
                   alpha, beta, Wg, W1, W2, W3, Ws1, Ws2, Ws3, out):
    F32, BF16, U32 = mybir.dt.float32, mybir.dt.bfloat16, mybir.dt.uint32
    ALU, ACT = mybir.AluOpType, mybir.ActivationFunctionType

    BATCH, LEN, C = x.shape
    E, _, H = W1.shape
    HS = Ws1.shape[1]
    DI = W_in.shape[1] // 2
    NS = A_log.shape[1]
    TAPS = conv_w.shape[2]
    P = 128
    NSEQ = 2
    TG = NSEQ * LEN
    TILES = TG // P
    G = BATCH // NSEQ
    HALVES = DI // P
    EH = E * H
    NCHUNK = -(-(EH + HS) // P)
    ECHUNK = EH // P
    LAST = EH + HS - (NCHUNK - 1) * P
    SLOTS = NS * HALVES
    PAD = TAPS - 1
    LN_EPS, STD_EPS = 1e-5, 1e-6
    PARTS = 3
    KP = 32 * PARTS
    ORDER = list(range(ECHUNK, NCHUNK)) + list(range(ECHUNK))

    def rows(j):
        return LAST if j == NCHUNK - 1 else P

    PLAN = {
        0: ["stats0", "gate_y", "norm0"], 1: ["outproj", "xT0", "x1n"], 2: ["outT"],
        3: ["resid_ln", "logits0"], 4: ["route0", "ln_scale"], 5: ["weights0", "wT0"], 6: ["ln_out"],
        8: ["stats1"], 9: ["norm1"], 10: ["xT1"], 11: ["logits1"], 12: ["route1"], 13: ["weights1"], 14: ["wT1"],
        18: ["yT0"], 19: ["addy0"], 20: ["stats2"], 21: ["norm2"], 22: ["xT2"],
        23: ["in0", "in1"], 24: ["in2", "in3"], 25: ["conv0"], 26: ["conv1"], 27: ["dt0", "dt1"],
        28: ["xproj"], 29: ["bcparts"], 30: ["delta"], 31: ["yT1", "addy1", "bcT"],
    }
    UP0, UP1 = 3, 17
    MISC_FIN = ["outproj", "outT"]
    MISC_FFN = [["xT0", "logits0", "wT0", "yT0"], ["xT1", "logits1", "wT1", "yT1"]]
    MISC_PREP = ["xT2", "in0", "in1", "in2", "in3", "dt0", "dt1", "xproj", "bcT"]

    def lead(k):
        return not isinstance(k, int) or k + 1 < G

    def scans(k):
        return not isinstance(k, int) or 0 <= k < G

    def tail(k):
        return not isinstance(k, int) or k >= 1

    def misc_list(k):
        names = (MISC_FFN[0] + MISC_PREP if lead(k) else []) + (MISC_FIN + MISC_FFN[1] if tail(k) else [])
        return [n for s in range(SLOTS) for n in PLAN.get(s, []) if n in names]

    N_FILL = [len(misc_list(-1)), len(misc_list(0))]
    N_FULL = len(misc_list(1))

    def turn(k, name):
        if not isinstance(k, int) or 1 <= k < G:
            base = sum(N_FILL) + (k - 1) * N_FULL
        elif k >= G:
            base = sum(N_FILL) + (G - 2) * N_FULL + len(misc_list(G - 1))
        else:
            base = sum(N_FILL[:k + 1])
        return base + misc_list(k).index(name) + 1

    def ffn_no(k, f):
        if isinstance(k, int) and k < 1:
            return k + 1
        if isinstance(k, int) and k >= G - 1:
            return 2 * (G - 1) + (k - (G - 1))
        return 2 * k + f

    def fcount(k, f, per, n):
        return ffn_no(k, f) * per + n

    def f_parity(k, f):
        return ffn_no(k, f) % 2 if isinstance(k, int) else f

    def up_unit(k, slot):
        if UP0 <= slot < UP0 + NCHUNK and lead(k):
            return 0, slot - UP0
        if UP1 <= slot < UP1 + NCHUNK and tail(k):
            return 1, slot - UP1
        return None

    def down_unit(k, slot):
        return up_unit(k, slot - 1) if slot else None

    def iterations(engine, body):
        body(-1, 1)
        body(0, 0)
        with engine.Fori(1, G - 1, 2) as k:
            body(k, 1)
            body(k + 1, 0)
        body(G - 1, 1)
        body(G, 0)

    ctx = ExitStack()
    with ctx:
        def sb(name, shape, dt=F32):
            return ctx.enter_context(nc.sbuf_tensor(name, shape, dt))

        def pb(name, shape=(P, TG)):
            return ctx.enter_context(nc.psum_tensor(name, list(shape), F32))

        def sem(name):
            return ctx.enter_context(nc.semaphore(name))

        XS = 4
        xres = sb("xres", [P, XS, TILES, C])
        up_w = sb("up_w", [P, 2, EH + HS])
        down_w = sb("down_w", [P, NCHUNK, C])
        wg = sb("wg", [P, E])
        w_in = sb("w_in", [P, 2 * DI])
        w_dt = sb("w_dt", [P, HALVES, DI])
        w_xp = sb("w_xp", [P, HALVES, 2 * NS])
        w_out = sb("w_out", [P, HALVES, C])
        b_in_c = sb("b_in_c", [P, 2 * HALVES])
        conv_w_c = sb("conv_w_c", [P, HALVES, TAPS])
        conv_b_c = sb("conv_b_c", [P, HALVES])
        b_dt_c = sb("b_dt_c", [P, HALVES])
        d_c = sb("d_c", [P, HALVES])
        b_out_c = sb("b_out_c", [P, 1])
        a_log = sb("a_log", [P, HALVES, NS])
        a_exp = sb("a_exp", [P, HALVES, NS])
        a_neg = sb("a_neg", [P, HALVES, NS])
        b_xp_b = sb("b_xp_b", [P, 2 * NS])
        alpha_b = sb("alpha_b", [P, C])
        beta_b = sb("beta_b", [P, C])
        ident = sb("ident", [P, P])
        ident_bf = sb("ident_bf", [P, P], BF16)
        sel_bc = sb("sel_bc", [KP, 2 * NS, P], BF16)
        sel_w = sb("sel_w", [KP, ECHUNK, P], BF16)
        pow_mhalf = sb("pow_mhalf", [P, TILES])
        pow_half = sb("pow_half", [P, TILES])
        euler = sb("euler", [P, TILES])
        lanes = sb("lanes", [P, TILES * 2, E])
        carrier = sb("carrier", [P, 1])
        bnst = sb("bnst", [P, 4, TILES, 6])
        mv = [sb(f"mv{f}", [P, TILES, 2]) for f in range(2)]
        mv1 = sb("mvx", [P, 2, TILES, 2])
        rstd1 = sb("rstdx", [P, 2, TILES])
        mvr = sb("mvr", [P, TILES, 2])
        varp = sb("varp", [P, 4, TILES])
        rstd = [sb(f"rstd{f}", [P, TILES]) for f in range(2)]
        stdr = sb("stdr", [P, 3, TILES])
        xn = [sb(f"xn{f}", [P, TILES, C]) for f in range(3)]
        xnT = [sb(f"xnT{f}", [P, TG]) for f in range(3)]
        logit = sb("logit", [P, TILES, E])
        top = sb("top", [P, TILES, 8])
        topi = sb("topi", [P, TILES, 8], U32)
        topf = sb("topf", [P, TILES, 2])
        drop = sb("drop", [P, TILES])
        edrop = sb("edrop", [P, TILES])
        den = sb("den", [P, TILES])
        prob = sb("prob", [P, TILES, 2])
        hot = sb("hot", [P, TILES, 2, E])
        hotp = sb("hotp", [P, TILES, 2, E])
        wtok = sb("wtok", [P, TILES, E])
        wrem = sb("wrem", [P, TILES, E])
        wrem2 = sb("wrem2", [P, TILES, E])
        wparts = sb("wparts", [P, TILES, KP], BF16)
        wT = [sb(f"wT{f}", [KP, TG], BF16) for f in range(2)]
        NSILU = 4
        silu = sb("silu", [P, NSILU, TG])
        mid = sb("mid", [P, 2, TG])
        gated = sb("gated", [P, 2, TG])
        yT = [sb(f"yT{f}", [P, TG]) for f in range(2)]
        xin = sb("xin", [P, HALVES, NSEQ, PAD + LEN])
        conv = sb("conv", [P, HALVES, NSEQ, LEN])
        xconv = [sb(f"xconv{i}", [P, HALVES, TG]) for i in range(2)]
        zs = [sb(f"zs{i}", [P, HALVES, TG]) for i in range(2)]
        dpre = sb("dpre", [P, HALVES, TG])
        dtmp = sb("dtmp", [P, HALVES, TG])
        delta = [sb(f"delta{i}", [P, HALVES, TG]) for i in range(2)]
        du = [sb(f"du{i}", [P, HALVES, TG]) for i in range(2)]
        bc = sb("bc", [P, TILES, 2 * NS])
        bcrem = sb("bcrem", [P, TILES, 2 * NS])
        bcrem2 = sb("bcrem2", [P, TILES, 2 * NS])
        bcparts = sb("bcparts", [P, TILES, KP], BF16)
        bcT = [sb(f"bcT{i}", [KP, TG], BF16) for i in range(2)]
        NA, NB, NH, NC = 8, 2, 4, 4
        decay = sb("decay", [P, NA, NSEQ, LEN])
        dbx = sb("dbx", [P, NB, TG])
        hist = sb("hist", [P, NH, TG])
        crow = sb("crow", [P, NC, TG])
        prod = sb("prod", [P, 2, TG])
        yacc = [sb(f"yacc{i}", [P, HALVES, TG]) for i in range(2)]
        yg = sb("yg", [P, HALVES, TG])
        oT = sb("oT", [P, TG])
        rtok = sb("rtok", [P, TILES, C])
        ps_h1 = [pb("ps_h1a"), pb("ps_h1b")]
        ps_h2, ps_wb, ps_y, ps_b, ps_c, ps_m = (pb(n) for n in ("ps_h2", "ps_wb", "ps_y", "ps_b", "ps_c", "ps_m"))

        consts_loaded = sem("consts_loaded")
        consts_made = sem("consts_made")
        a_exped = sem("a_exped")
        a_ready = sem("a_ready")
        pads_zero = sem("pads_zero")
        x_loaded = sem("x_loaded")
        x_stored = sem("x_stored")
        misc_full = sem("misc_full")
        misc_taken = sem("misc_taken")
        var_ready = [sem(f"var_ready{i}") for i in range(4)]
        rstd_ready = [sem(f"rstd_ready{i}") for i in range(4)]
        norm_ready = [sem(f"norm_ready{i}") for i in range(3)]
        drop_ready = sem("drop_ready")
        edrop_ready = sem("edrop_ready")
        wparts_ready = sem("wparts_ready")
        h1_full, h2_full = sem("h1_full"), sem("h2_full")
        silu_done, mid_done, gate_done, down_done = sem("silu_done"), sem("mid_done"), sem("gate_done"), sem("down_done")
        y_taken = sem("y_taken")
        xin_ready, conv_ready, xconv_ready = sem("xin_ready"), sem("conv_ready"), sem("xconv_ready")
        zs_ready, logterm_ready, softplus_chain = sem("zs_ready"), sem("logterm_ready"), sem("softplus_chain")
        delta_ready, du_ready, bcparts_ready = sem("delta_ready"), sem("du_ready"), sem("bcparts_ready")
        decay_ready, b_full, c_full, crow_ready = sem("decay_ready"), sem("b_full"), sem("c_full"), sem("crow_ready")
        dbx_done, scan_done, prod_done, acc_done = sem("dbx_done"), sem("scan_done"), sem("prod_done"), sem("acc_done")
        yg_ready = sem("yg_ready")
        x_added = sem("x_added")
        dve_stats, dve_route, dve_conv, dve_bc, dve_fin = (sem(n) for n in (
            "dve_stats", "dve_route", "dve_conv", "dve_bc", "dve_fin"))

        class Chain:

            def __init__(self, engine, sem, per, number):
                self.engine, self.sem, self.per, self.at, self.n = engine, sem, per, number * per, 0

            def link(self, ins):
                self.n += 1
                ins.then_inc(self.sem, 1)
                self.engine.wait_ge(self.sem, self.at + self.n)

            def end(self):
                assert self.n == self.per, (self.n, self.per)

        N_CONSTS, N_MADE = 22, 19
        ROUTE_LINKS, FIN_LINKS = 13, 7
        block = ctx.enter_context(nc.Block())

        @block.sync
        def _(sp):
            def load(g, slot):
                sp.dma_start(xres[:, slot, :, :],
                             x[bass.ds(g * NSEQ, NSEQ)].rearrange("b (t p) c -> p (b t) c", p=P)).then_inc(x_loaded, 16)

            def store(g, slot, k):
                sp.wait_ge(misc_taken, turn(k, "yT1"))
                sp.wait_ge(x_loaded, 16 * min(g + XS, G) if isinstance(k, int) else 16 * (g + XS))
                sp.dma_start(out[bass.ds(g * NSEQ, NSEQ)].rearrange("b (t p) c -> p (b t) c", p=P),
                             xres[:, slot, :, :]).then_inc(x_stored, 16)
                sp.wait_ge(x_stored, 16 * (g + 1))

            for g in range(XS):
                load(g, g)
                sp.wait_ge(x_loaded, 16 * (g + 1))
            with sp.Fori(1, G - XS + 1) as k:
                store(k - 1, (k - 1) % XS, k)
                load(k - 1 + XS, (k - 1) % XS)
            for k in range(G - XS + 1, G + 1):
                store(k - 1, (k - 1) % XS, k)

        @block.gpsimd
        def _(pool):
            made = 0

            def made_one(ins):
                nonlocal made
                made += 1
                ins.then_inc(consts_made, 1)
                pool.wait_ge(consts_made, made)

            made_one(nc.gpsimd.memset(ident[:], 0.0))
            made_one(nc.gpsimd.memset(ident_bf[:], 0.0))
            made_one(nc.gpsimd.memset(sel_bc[:], 0.0))
            made_one(nc.gpsimd.memset(sel_w[:], 1.0))
            made_one(nc.gpsimd.memset(pow_mhalf[:], -0.5))
            made_one(nc.gpsimd.memset(pow_half[:], 0.5))
            made_one(nc.gpsimd.memset(euler[:], math.e))
            made_one(nc.gpsimd.iota(lanes[:], [[0, TILES * 2], [1, E]], base=0, channel_multiplier=0,
                                    allow_small_or_imprecise_dtypes=True))
            for m in (ident, ident_bf):
                made_one(nc.gpsimd.affine_select(out=m[:], in_=m[:], compare_op=ALU.not_equal, fill=1.0, base=0,
                                                 pattern=[[-1, P]], channel_multiplier=1))
            for q in range(PARTS):
                part = sel_bc[32 * q:32 * q + 32, :, :]
                made_one(nc.gpsimd.affine_select(out=part, in_=part, compare_op=ALU.not_equal, fill=1.0, base=0,
                                                 pattern=[[-1, 2 * NS], [0, P]], channel_multiplier=1))
                part = sel_w[32 * q:32 * q + 32, :, :]
                made_one(nc.gpsimd.affine_select(out=part, in_=part, compare_op=ALU.is_ge, fill=0.0, base=0,
                                                 pattern=[[P, ECHUNK], [1, P]], channel_multiplier=-H))
            for q in range(PARTS):
                part = sel_w[32 * q:32 * q + 32, :, :]
                made_one(nc.gpsimd.affine_select(out=part, in_=part, compare_op=ALU.is_ge, fill=0.0, base=H - 1,
                                                 pattern=[[-P, ECHUNK], [-1, P]], channel_multiplier=H))

            def power(dst, src, exponent, ready, done, value):
                pool.wait_ge(ready, value)
                nc.gpsimd.tensor_tensor(dst, src, exponent, ALU.pow).then_inc(done, 1)

            def body(k, odd):
                for slot in range(SLOTS):
                    for step in PLAN.get(slot, []):
                        if step == "stats0" and lead(k):
                            power(rstd[0][:], varp[:, 0, :], pow_mhalf[:], var_ready[0], rstd_ready[0], k + 2)
                        elif step == "stats1" and tail(k):
                            power(rstd[1][:], varp[:, 1, :], pow_mhalf[:], var_ready[1], rstd_ready[1], k)
                        elif step == "stats2" and lead(k):
                            power(rstd1[:, 1 - odd, :], varp[:, 2, :], pow_mhalf[:], var_ready[2],
                                  rstd_ready[2], k + 2)
                        elif step == "resid_ln" and tail(k):
                            power(stdr[:, 0, :], varp[:, 3, :], pow_half[:], var_ready[3], rstd_ready[3], k)
                        elif (step == "route0" and lead(k)) or (step == "route1" and tail(k)):
                            n = ffn_no(k, int(step == "route1")) + 1
                            pool.wait_ge(drop_ready, n)
                            nc.gpsimd.tensor_tensor(edrop[:], euler[:], drop[:], ALU.pow).then_inc(edrop_ready, 1)
                    if scans(k):
                        s, half = divmod(slot, HALVES)
                        m = SLOTS * k + slot
                        pool.wait_ge(scan_done, m + 1)
                        pool.wait_ge(crow_ready, NS * k + s + 1)
                        if s == 0:
                            nc.gpsimd.tensor_tensor(yacc[odd][:, half, :],
                                                    hist[:, slot % NH, :], crow[:, s % NC, :], ALU.mult
                                                    ).then_inc(prod_done, 1)
                        else:
                            if slot > 3 or not isinstance(k, int) or k > 0:
                                pool.wait_ge(acc_done, (SLOTS - HALVES) * k + slot - 3)
                            nc.gpsimd.tensor_tensor(prod[:, slot % 2, :], hist[:, slot % NH, :], crow[:, s % NC, :],
                                                    ALU.mult).then_inc(prod_done, 1)
                        if slot > HALVES:
                            accumulate(k, odd, slot - 1)
                        if slot == SLOTS - 1:
                            accumulate(k, odd, slot)

            def accumulate(k, odd, slot):
                half = slot % HALVES
                pool.wait_ge(prod_done, SLOTS * k + slot + 1)
                if slot >= 2 * HALVES:
                    pool.wait_ge(acc_done, (SLOTS - HALVES) * k + slot - HALVES - 1)
                y = yacc[odd][:, half, :]
                nc.gpsimd.tensor_tensor(y, y, prod[:, slot % 2, :], ALU.add).then_inc(acc_done, 1)

            iterations(pool, body)

        @block.scalar
        def _(act):
            n_const = 0

            def const(dst, src):
                nonlocal n_const
                n_const += 1
                act.dma_start(dst, src).then_inc(consts_loaded, 16)

            with nc.allow_non_contiguous_dma(reason="small constants in column form"):
                const(a_log[:], A_log.rearrange("(h p) s -> p h s", p=P))
                const(wg[:], Wg[:, :])
                for i, (we, ws) in enumerate(((W1, Ws1), (W2, Ws2))):
                    const(up_w[:, i, 0:EH].rearrange("c (e h) -> c e h", e=E), we.rearrange("e c h -> c e h"))
                    const(up_w[:, i, EH:EH + HS], ws[:, :])
                const(down_w[:, 0:ECHUNK, :], W3.rearrange("e h c -> (e h) c").rearrange("(j p) c -> p j c", p=P))
                full = HS // P
                const(down_w[:, ECHUNK:ECHUNK + full, :], Ws3[0:full * P, :].rearrange("(j p) c -> p j c", p=P))
                const(down_w[0:LAST, NCHUNK - 1, :], Ws3[full * P:HS, :])
                const(w_in[:], W_in[:, :])
                const(w_dt[:], W_dt.rearrange("(h p) n -> p h n", p=P))
                const(w_xp[:], W_xp.rearrange("(h p) n -> p h n", p=P))
                const(w_out[:], W_out.rearrange("(h p) n -> p h n", p=P))
                const(b_in_c[:], b_in.rearrange("(h p) -> p h", p=P))
                const(conv_w_c[:], conv_w.rearrange("(h p) o t -> p h (o t)", p=P))
                const(conv_b_c[:], conv_b.rearrange("(h p) -> p h", p=P))
                const(b_dt_c[:], b_dt.rearrange("(h p) -> p h", p=P))
                const(d_c[:], D_skip.rearrange("(h p) -> p h", p=P))
                const(b_out_c[:], b_out.rearrange("(h p) -> p h", p=P))
                const(b_xp_b[:], b_xp.partition_broadcast(P))
                const(alpha_b[:], alpha.partition_broadcast(P))
                const(beta_b[:], beta.partition_broadcast(P))
            assert n_const == N_CONSTS, n_const
            act.wait_ge(consts_loaded, 16 * n_const)
            nc.scalar.activation(a_exp[:], a_log[:], ACT.Exp).then_inc(a_exped, 1)
            act.wait_ge(a_ready, 1)
            act.wait_ge(pads_zero, 5)

            def take(k, name):
                act.wait_ge(misc_full, turn(k, name))

            def decays(k, odd, units):
                for slot in units:
                    s, half = divmod(slot, HALVES)
                    m = SLOTS * k + slot
                    if slot >= NA:
                        act.wait_ge(scan_done, m - NA + 1)
                    elif not isinstance(k, int) or k > 0:
                        act.wait_ge(scan_done, m - NA + 1)
                    if slot == 0:
                        act.wait_ge(delta_ready, k + 1)
                    d = delta[odd][:, half, :].rearrange("p (b t) -> p b t", b=NSEQ)
                    nc.scalar.activation(decay[:, slot % NA, :, 1:LEN], d[:, :, 1:LEN], ACT.Exp,
                                         scale=a_neg[:, half, s:s + 1]).then_inc(decay_ready, 1)

            def body(k, odd):
                nxt = 1 - odd
                for slot in range(SLOTS):
                    if scans(k):
                        if slot == 0:
                            decays(k, odd, range(NA))
                        elif slot % 4 == 0 and slot + 4 < SLOTS:
                            decays(k, odd, range(slot + 4, slot + 8))
                        if slot % HALVES == 0:
                            s = slot // HALVES
                            act.wait_ge(c_full, NS * k + s + 1)
                            if s >= NC:
                                act.wait_ge(prod_done, SLOTS * k + HALVES * (s - NC + 1))
                            elif not isinstance(k, int) or k > 0:
                                act.wait_ge(prod_done, SLOTS * k + HALVES * (s - NC + 1))
                            nc.scalar.activation(crow[:, s % NC, :], ps_c[:], ACT.Copy).then_inc(crow_ready, 1)
                    u = up_unit(k, slot)
                    if u is not None:
                        f, pos = u
                        r = rows(ORDER[pos])
                        n = fcount(k, f, NCHUNK, pos)
                        act.wait_ge(h1_full, n + 1)
                        if not isinstance(n, int) or n >= NSILU:
                            act.wait_ge(gate_done, n - NSILU + 1)
                        place = (pos + NCHUNK * f_parity(k, f)) % NSILU
                        nc.scalar.activation(silu[0:r, place, :], ps_h1[pos % 2][0:r, :],
                                             ACT.Silu).then_inc(silu_done, 1)
                    for step in PLAN.get(slot, []):
                        if step in ("xT0", "xT2") and lead(k) or step == "xT1" and tail(k):
                            take(k, step)
                            nc.scalar.activation(xnT[int(step[2])][:], ps_m[:], ACT.Copy).then_inc(misc_taken, 1)
                        elif step == "wT0" and lead(k) or step == "wT1" and tail(k):
                            take(k, step)
                            nc.scalar.activation(wT[int(step[2])][:], ps_m[0:KP, 0:TG // 2].bitcast(BF16),
                                                 ACT.Copy).then_inc(misc_taken, 1)
                        elif step == "bcT" and lead(k):
                            take(k, step)
                            nc.scalar.activation(bcT[nxt][:], ps_m[0:KP, 0:TG // 2].bitcast(BF16),
                                                 ACT.Copy).then_inc(misc_taken, 1)
                        elif step == "yT0" and lead(k) or step == "yT1" and tail(k):
                            f = int(step[2])
                            act.wait_ge(down_done, fcount(k, f, NCHUNK, NCHUNK))
                            nc.scalar.activation(yT[f][:], ps_y[:], ACT.Copy).then_inc(y_taken, 1)
                        elif step == "outproj" and tail(k):
                            take(k, step)
                            nc.scalar.activation(oT[:], ps_m[:], ACT.Identity,
                                                 bias=b_out_c[:, 0:1]).then_inc(misc_taken, 1)
                        elif step in ("in0", "in1") and lead(k):
                            half = int(step[2])
                            take(k, step)
                            nc.scalar.activation(xin[:, half, :, PAD:PAD + LEN],
                                                 ps_m[:].rearrange("p (b t) -> p b t", b=NSEQ), ACT.Identity,
                                                 bias=b_in_c[:, half:half + 1]).then_inc(misc_taken, 1)
                        elif step in ("in2", "in3") and lead(k):
                            half = int(step[2]) - HALVES
                            take(k, step)
                            nc.scalar.activation(zs[nxt][:, half, :], ps_m[:], ACT.Silu,
                                                 bias=b_in_c[:, HALVES + half:HALVES + half + 1]
                                                 ).then_inc(misc_taken, 1)
                        elif step in ("conv0", "conv1") and lead(k):
                            half = int(step[4])
                            act.wait_ge(conv_ready, HALVES * (k + 1) + half + 1)
                            nc.scalar.activation(xconv[nxt][:, half, :],
                                                 conv[:, half, :, :].rearrange("p b t -> p (b t)"), ACT.Silu,
                                                 bias=conv_b_c[:, half:half + 1]).then_inc(xconv_ready, 1)
                        elif step in ("dt0", "dt1") and lead(k):
                            half = int(step[2])
                            take(k, step)
                            nc.scalar.activation(dpre[:, half, :], ps_m[:], ACT.Identity,
                                                 bias=b_dt_c[:, half:half + 1]).then_inc(misc_taken, 1)
                            if half == HALVES - 1:
                                act.wait_ge(misc_taken, turn(k, "dt1"))
                                chain = Chain(act, softplus_chain, 2, k + 1)
                                chain.link(nc.scalar.activation(dtmp[:], dpre[:], ACT.Abs))
                                chain.link(nc.scalar.activation(dtmp[:], dtmp[:], ACT.Exp, scale=-1.0))
                                chain.end()
                                nc.scalar.activation(dtmp[:], dtmp[:], ACT.Ln, bias=1.0).then_inc(logterm_ready, 1)

            iterations(act, body)

        @block.vector
        def _(dve):
            nc.vector.memset(xin[:, :, :, 0:PAD], 0.0).then_inc(pads_zero, 1)
            nc.vector.memset(decay[:, :, :, 0:1], 0.0).then_inc(pads_zero, 1)
            nc.vector.memset(wparts[:], 0.0).then_inc(pads_zero, 1)
            nc.vector.memset(bcparts[:], 0.0).then_inc(pads_zero, 1)
            dve.wait_ge(a_exped, 1)
            nc.vector.tensor_scalar(a_neg[:], a_exp[:], -1.0, None, ALU.mult).then_inc(a_ready, 1)
            nc.vector.memset(mid[:], 0.0).then_inc(pads_zero, 1)
            dve.wait_ge(consts_loaded, 16 * N_CONSTS)
            dve.wait_ge(consts_made, N_MADE)
            dve.wait_ge(pads_zero, 5)

            def plain_wait():
                dve.wait_ge(pads_zero, 5)

            def statistics(src, which, agg, signal_n, number, scale, shift):
                chain = Chain(dve, dve_stats, 2, number)
                for t in range(TILES):
                    ins = nc.vector.bn_stats(bnst[:, which, t, :], src[:, t, :])
                chain.link(ins)
                nc.vector.memset(carrier[:], 0.0)
                for t in range(TILES):
                    ins = nc.vector.bn_aggr(agg[:, t, :], bnst[:, which, t, :])
                chain.link(ins)
                chain.end()
                nc.vector.tensor_scalar(varp[:, which, :], agg[:, :, 1], scale, shift, ALU.mult, ALU.add
                                        ).then_inc(var_ready[which], 1)

            def stats_no(k, which):
                names = {"stats0": 0, "resid_ln": 3, "stats1": 1, "stats2": 2}
                def here(kk):
                    return [names[n] for s in range(SLOTS) for n in PLAN.get(s, []) if n in names
                            and (lead(kk) if n in ("stats0", "stats2") else tail(kk))]
                if isinstance(k, int) and k < 1:
                    base = len(here(-1)) * (k + 1)
                elif isinstance(k, int) and k == G:
                    base = 2 * len(here(-1)) + (G - 2) * 4 + len(here(G - 1))
                else:
                    base = 2 * len(here(-1)) + (k - 1) * 4
                return base + here(k).index(which)

            def normalise(dst, src, agg, inv):
                for t in range(TILES):
                    ins = nc.vector.tensor_scalar(dst[:, t, :], src[:, t, :], agg[:, t, 0:1], inv[:, t:t + 1],
                                                  ALU.subtract, ALU.mult)
                return ins

            def split(chain, whole, rem, rem2, parts, width):
                hi, md, lo = (parts[:, :, 32 * q:32 * q + width] for q in range(PARTS))
                chain.link(nc.vector.tensor_copy(hi, whole))
                chain.link(nc.vector.tensor_tensor(rem, whole, hi, ALU.subtract))
                chain.link(nc.vector.tensor_copy(md, rem))
                chain.link(nc.vector.tensor_tensor(rem2, rem, md, ALU.subtract))
                return nc.vector.tensor_copy(lo, rem2)

            route_chain = fin_chain = None

            def body(k, odd):
                nonlocal route_chain, fin_chain
                nxt = 1 - odd
                ahead, behind = (k + 1) % XS, (k - 1) % XS if tail(k) else 0
                for slot in range(SLOTS):
                    if scans(k):
                        s, half = divmod(slot, HALVES)
                        m = SLOTS * k + slot
                        dve.wait_ge(b_full, NS * k + s + 1)
                        if slot == 0:
                            dve.wait_ge(du_ready, k + 1)
                        nc.vector.tensor_tensor(dbx[:, slot % NB, :], du[odd][:, half, :], ps_b[:], ALU.mult
                                                ).then_inc(dbx_done, 1)
                    d = down_unit(k, slot)
                    if d is not None:
                        f, pos = d
                        j = ORDER[pos]
                        r = rows(j)
                        n = fcount(k, f, NCHUNK, pos)
                        place = (pos + NCHUNK * f_parity(k, f)) % NSILU
                        dve.wait_ge(silu_done, n + 1)
                        dve.wait_ge(h2_full, n + 1)
                        if j >= ECHUNK:
                            if not isinstance(n, int) or n >= 2:
                                dve.wait_ge(down_done, n - 1)
                            nc.vector.tensor_tensor(gated[0:r, pos % 2, :], silu[0:r, place, :], ps_h2[0:r, :],
                                                    ALU.mult).then_inc(gate_done, 1)
                        else:
                            nc.vector.tensor_tensor(mid[:, pos % 2, :], silu[:, place, :], ps_h2[:], ALU.mult
                                                    ).then_inc(mid_done, 1)
                    if scans(k):
                        dve.wait_ge(dbx_done, m + 1)
                        dve.wait_ge(decay_ready, m + 1)
                        if slot >= NH or not isinstance(k, int) or k > 0:
                            dve.wait_ge(prod_done, m - NH + 1)
                        nc.vector.tensor_tensor_scan(hist[:, slot % NH, :],
                                                     decay[:, slot % NA, :, :].rearrange("p b t -> p (b t)"),
                                                     dbx[:, slot % NB, :], 0.0, ALU.mult, ALU.add
                                                     ).then_inc(scan_done, 1)
                    if d is not None and j < ECHUNK:
                        dve.wait_ge(mid_done, fcount(k, f, ECHUNK, pos - (NCHUNK - ECHUNK) + 1))
                        dve.wait_ge(down_done, n - 1)
                        nc.vector.tensor_tensor(gated[:, pos % 2, :], mid[:, pos % 2, :], ps_wb[:], ALU.mult
                                                ).then_inc(gate_done, 1)
                    for step in PLAN.get(slot, []):
                        if step == "stats0" and lead(k):
                            plain_wait()
                            dve.wait_ge(x_loaded, 16 * (k + 2))
                            statistics(xres[:, ahead, :, :], 0, mv[0], 0, stats_no(k, 0), 1.0, LN_EPS)
                        elif step == "stats1" and tail(k):
                            plain_wait()
                            dve.wait_ge(x_added, k)
                            statistics(xres[:, behind, :, :], 1, mv[1], 1, stats_no(k, 1), 1.0, LN_EPS)
                        elif step == "stats2" and lead(k):
                            plain_wait()
                            dve.wait_ge(misc_taken, turn(k, "yT0"))
                            statistics(xres[:, ahead, :, :], 2, mv1[:, nxt, :, :], 2, stats_no(k, 2), 1.0, LN_EPS)
                        elif step == "norm0" and lead(k):
                            dve.wait_ge(rstd_ready[0], k + 2)
                            normalise(xn[0], xres[:, ahead, :, :], mv[0], rstd[0]).then_inc(norm_ready[0], 1)
                        elif step == "norm1" and tail(k):
                            dve.wait_ge(rstd_ready[1], k)
                            normalise(xn[1], xres[:, behind, :, :], mv[1], rstd[1]).then_inc(norm_ready[1], 1)
                        elif step == "norm2" and lead(k):
                            dve.wait_ge(rstd_ready[2], k + 2)
                            normalise(xn[2], xres[:, ahead, :, :], mv1[:, nxt, :, :], rstd1[:, nxt, :]
                                      ).then_inc(norm_ready[2], 1)
                        elif step == "route0" and lead(k) or step == "route1" and tail(k):
                            f = int(step[5])
                            dve.wait_ge(misc_full, turn(k, f"logits{f}"))
                            nc.vector.tensor_copy(logit[:], ps_m[:, 0:TILES * E].rearrange("p (t e) -> p t e", e=E)
                                                  ).then_inc(misc_taken, 1)
                            plain_wait()
                            dve.wait_ge(misc_taken, turn(k, f"logits{f}"))
                            chain = Chain(dve, dve_route, ROUTE_LINKS, ffn_no(k, f))
                            for t in range(TILES):
                                ins = nc.vector.max(top[:, t, :], logit[:, t, :])
                            chain.link(ins)
                            nc.vector.tensor_tensor(drop[:], top[:, :, 1], top[:, :, 0], ALU.subtract
                                                    ).then_inc(drop_ready, 1)
                            for t in range(TILES):
                                ins = nc.vector.max_index(topi[:, t, :], top[:, t, :], logit[:, t, :])
                            chain.link(ins)
                            chain.link(nc.vector.tensor_copy(topf[:], topi[:, :, 0:2]))
                            chain.link(nc.vector.tensor_tensor(
                                hot[:].rearrange("p t i e -> p (t i) e"), lanes[:],
                                topf[:].rearrange("p t i -> p (t i)").unsqueeze(2).to_broadcast([P, TILES * 2, E]),
                                ALU.is_equal))
                            route_chain = chain
                        elif step == "weights0" and lead(k) or step == "weights1" and tail(k):
                            f = int(step[7])
                            chain = route_chain
                            dve.wait_ge(edrop_ready, ffn_no(k, f) + 1)
                            chain.link(nc.vector.tensor_scalar(den[:], edrop[:], 1.0, None, ALU.add))
                            chain.link(nc.vector.reciprocal(prob[:, :, 0], den[:]))
                            chain.link(nc.vector.tensor_tensor(prob[:, :, 1], edrop[:], prob[:, :, 0], ALU.mult))
                            chain.link(nc.vector.tensor_tensor(
                                hotp[:].rearrange("p t i e -> p (t i) e"), hot[:].rearrange("p t i e -> p (t i) e"),
                                prob[:].rearrange("p t i -> p (t i)").unsqueeze(2).to_broadcast([P, TILES * 2, E]),
                                ALU.mult))
                            chain.link(nc.vector.tensor_tensor(wtok[:], hotp[:, :, 0, :], hotp[:, :, 1, :], ALU.add))
                            split(chain, wtok[:], wrem[:], wrem2[:], wparts, E).then_inc(wparts_ready, 1)
                            chain.end()
                        elif step == "yT0" and lead(k) or step == "yT1" and tail(k):
                            pass
                        elif step == "addy0" and lead(k) or step == "addy1" and tail(k):
                            f = int(step[4])
                            dve.wait_ge(misc_full, turn(k, f"yT{f}"))
                            xr = xres[:, behind if f else ahead, :, :].rearrange("p t c -> p (t c)")
                            nc.vector.scalar_tensor_tensor(xr, ps_m[:], 0.5, xr, ALU.mult, ALU.add
                                                           ).then_inc(misc_taken, 1)
                        elif step in ("conv0", "conv1") and lead(k):
                            half = int(step[4])
                            acc = conv[:, half, :, :]
                            dve.wait_ge(misc_taken, turn(k, f"in{half}"))
                            chain = Chain(dve, dve_conv, TAPS - 1, HALVES * (k + 1) + half)
                            ins = nc.vector.tensor_scalar(acc, xin[:, half, :, 0:LEN], conv_w_c[:, half, 0:1], None,
                                                          ALU.mult)
                            for tap in range(1, TAPS):
                                chain.link(ins)
                                ins = nc.vector.scalar_tensor_tensor(acc, xin[:, half, :, tap:tap + LEN],
                                                                     conv_w_c[:, half, tap:tap + 1], acc,
                                                                     ALU.mult, ALU.add)
                            chain.end()
                            ins.then_inc(conv_ready, 1)
                        elif step == "delta" and lead(k):
                            dve.wait_ge(logterm_ready, k + 2)
                            nc.vector.scalar_tensor_tensor(delta[nxt][:], dpre[:], 0.0, dtmp[:], ALU.max, ALU.add
                                                           ).then_inc(delta_ready, 1)
                            dve.wait_ge(delta_ready, k + 2)
                            nc.vector.tensor_tensor(du[nxt][:], delta[nxt][:], xconv[nxt][:], ALU.mult
                                                    ).then_inc(du_ready, 1)
                        elif step == "bcparts" and lead(k):
                            dve.wait_ge(misc_full, turn(k, "xproj"))
                            nc.vector.tensor_tensor(
                                bc[:], ps_m[:, 0:TILES * 2 * NS].rearrange("p (t n) -> p t n", t=TILES),
                                b_xp_b[:].unsqueeze(1).to_broadcast([P, TILES, 2 * NS]), ALU.add
                            ).then_inc(misc_taken, 1)
                            dve.wait_ge(misc_taken, turn(k, "xproj"))
                            chain = Chain(dve, dve_bc, 4, k + 1)
                            split(chain, bc[:], bcrem[:], bcrem2[:], bcparts, 2 * NS).then_inc(bcparts_ready, 1)
                            chain.end()
                        elif step == "gate_y" and tail(k):
                            dve.wait_ge(acc_done, (SLOTS - HALVES) * k)
                            chain = Chain(dve, dve_fin, FIN_LINKS, k - 1)
                            for half in range(HALVES):
                                ins = nc.vector.scalar_tensor_tensor(yg[:, half, :], xconv[nxt][:, half, :],
                                                                     d_c[:, half:half + 1], yacc[nxt][:, half, :],
                                                                     ALU.mult, ALU.add)
                            chain.link(ins)
                            nc.vector.tensor_tensor(yg[:], yg[:], zs[nxt][:], ALU.mult).then_inc(yg_ready, 1)
                            fin_chain = chain
                        elif step == "x1n" and tail(k):
                            normalise(rtok, xres[:, behind, :, :], mv1[:, nxt, :, :], rstd1[:, nxt, :]
                                      ).then_inc(dve_fin, 1)
                            fin_chain.n += 1
                            dve.wait_ge(dve_fin, fin_chain.at + fin_chain.n)
                        elif step == "resid_ln" and tail(k):
                            dve.wait_ge(misc_full, turn(k, "outT"))
                            r2 = rtok[:].rearrange("p t c -> p (t c)")
                            nc.vector.tensor_tensor(r2, r2, ps_m[:], ALU.add).then_inc(misc_taken, 1)
                            plain_wait()
                            dve.wait_ge(misc_taken, turn(k, "outT"))
                            statistics(rtok, 3, mvr, 3, stats_no(k, 3), C / (C - 1), 0.0)
                        elif step == "ln_scale" and tail(k):
                            chain = fin_chain
                            dve.wait_ge(rstd_ready[3], k)
                            chain.link(nc.vector.tensor_scalar(stdr[:, 1, :], stdr[:, 0, :], STD_EPS, None, ALU.add))
                            chain.link(nc.vector.reciprocal(stdr[:, 2, :], stdr[:, 1, :]))
                            chain.link(normalise(rtok, rtok, mvr, stdr[:, 2, :]))
                            chain.link(nc.vector.tensor_tensor(rtok[:], rtok[:],
                                                               alpha_b[:].unsqueeze(1).to_broadcast([P, TILES, C]),
                                                               ALU.mult))
                            chain.link(nc.vector.tensor_tensor(rtok[:], rtok[:],
                                                               beta_b[:].unsqueeze(1).to_broadcast([P, TILES, C]),
                                                               ALU.add))
                            chain.end()
                        elif step == "ln_out" and tail(k):
                            nc.vector.tensor_tensor(xres[:, behind, :, :], xres[:, behind, :, :], rtok[:], ALU.add
                                                    ).then_inc(x_added, 1)

            iterations(dve, body)

        @block.tensor
        def _(pe):
            pe.wait_ge(consts_loaded, 16 * N_CONSTS)
            pe.wait_ge(consts_made, N_MADE)

            def claim(k, name):
                n = turn(k, name) - 1
                if not isinstance(n, int) or n > 0:
                    pe.wait_ge(misc_taken, n)

            def to_rows(src, width, idn, dst):
                for t in range(TILES):
                    ins = nc.tensor.transpose(dst[0:width, t * P:(t + 1) * P], src[:, t, :] if len(src.shape) == 3
                                              else src[:, t * P:(t + 1) * P], idn[:])
                return ins

            def body(k, odd):
                nxt = 1 - odd
                for slot in range(SLOTS):
                    if scans(k) and slot % HALVES == 0:
                        s = slot // HALVES
                        if slot == 0:
                            pe.wait_ge(misc_taken, turn(k - 1, "bcT"))
                        if slot or not isinstance(k, int) or k > 0:
                            pe.wait_ge(dbx_done, SLOTS * k + slot)
                            pe.wait_ge(crow_ready, NS * k + s)
                        nc.tensor.matmul(ps_b[:], sel_bc[:, s, :], bcT[odd][:], start=True, stop=True
                                         ).then_inc(b_full, 1)
                        nc.tensor.matmul(ps_c[:], sel_bc[:, NS + s, :], bcT[odd][:], start=True, stop=True
                                         ).then_inc(c_full, 1)
                    u = up_unit(k, slot)
                    if u is not None:
                        f, pos = u
                        j = ORDER[pos]
                        r = rows(j)
                        n = fcount(k, f, NCHUNK, pos)
                        if pos == 0:
                            pe.wait_ge(misc_taken, turn(k, f"xT{f}"))
                        if not isinstance(n, int) or n >= 2:
                            pe.wait_ge(silu_done, n - 1)
                        nc.tensor.matmul(ps_h1[pos % 2][0:r, :], up_w[:, 0, j * P:j * P + r], xnT[f][:],
                                         start=True, stop=True).then_inc(h1_full, 1)
                        if not isinstance(n, int) or n >= 1:
                            pe.wait_ge(gate_done, n)
                        if j < ECHUNK:
                            if j == 0:
                                pe.wait_ge(misc_taken, turn(k, f"wT{f}"))
                            nc.tensor.matmul(ps_wb[:], sel_w[:, j, :], wT[f][:], start=True, stop=True)
                        nc.tensor.matmul(ps_h2[0:r, :], up_w[:, 1, j * P:j * P + r], xnT[f][:],
                                         start=True, stop=True).then_inc(h2_full, 1)
                    d = down_unit(k, slot)
                    if d is not None:
                        f, pos = d
                        j = ORDER[pos]
                        r = rows(j)
                        pe.wait_ge(gate_done, fcount(k, f, NCHUNK, pos + 1))
                        if pos == 0 and (not isinstance(k, int) or k >= 0):
                            pe.wait_ge(y_taken, ffn_no(k, f))
                        nc.tensor.matmul(ps_y[:], down_w[0:r, j, :], gated[0:r, pos % 2, :], start=(pos == 0),
                                         stop=(pos == NCHUNK - 1)).then_inc(down_done, 1)
                    for step in PLAN.get(slot, []):
                        if step in ("xT0", "xT2") and lead(k) or step == "xT1" and tail(k):
                            f = int(step[2])
                            pe.wait_ge(norm_ready[f], k if f == 1 else k + 2)
                            claim(k, step)
                            to_rows(xn[f], P, ident, ps_m).then_inc(misc_full, 1)
                        elif step == "logits0" and lead(k) or step == "logits1" and tail(k):
                            f = int(step[6])
                            claim(k, step)
                            for t in range(TILES):
                                ins = nc.tensor.matmul(ps_m[:, t * E:(t + 1) * E], xnT[f][:, t * P:(t + 1) * P],
                                                       wg[:], start=True, stop=True)
                            ins.then_inc(misc_full, 1)
                        elif step == "wT0" and lead(k) or step == "wT1" and tail(k):
                            pe.wait_ge(wparts_ready, ffn_no(k, int(step[2])) + 1)
                            claim(k, step)
                            to_rows(wparts, KP, ident_bf, ps_m[:, 0:TG // 2].bitcast(BF16)).then_inc(misc_full, 1)
                        elif step == "bcT" and lead(k):
                            pe.wait_ge(bcparts_ready, k + 2)
                            claim(k, step)
                            to_rows(bcparts, KP, ident_bf, ps_m[:, 0:TG // 2].bitcast(BF16)).then_inc(misc_full, 1)
                        elif step == "yT0" and lead(k) or step == "yT1" and tail(k):
                            f = int(step[2])
                            pe.wait_ge(y_taken, ffn_no(k, f) + 1)
                            claim(k, step)
                            to_rows(yT[f], P, ident, ps_m).then_inc(misc_full, 1)
                        elif step in ("in0", "in1", "in2", "in3") and lead(k):
                            c = int(step[2])
                            claim(k, step)
                            nc.tensor.matmul(ps_m[:], w_in[:, c * P:(c + 1) * P], xnT[2][:], start=True, stop=True
                                             ).then_inc(misc_full, 1)
                        elif step in ("dt0", "dt1") and lead(k):
                            c = int(step[2])
                            pe.wait_ge(xconv_ready, HALVES * (k + 2))
                            claim(k, step)
                            for half in range(HALVES):
                                ins = nc.tensor.matmul(ps_m[:], w_dt[:, half, c * P:(c + 1) * P],
                                                       xconv[nxt][:, half, :], start=(half == 0),
                                                       stop=(half == HALVES - 1))
                            ins.then_inc(misc_full, 1)
                        elif step == "xproj" and lead(k):
                            claim(k, step)
                            for t in range(TILES):
                                for half in range(HALVES):
                                    ins = nc.tensor.matmul(ps_m[:, t * 2 * NS:(t + 1) * 2 * NS],
                                                           xconv[nxt][:, half, t * P:(t + 1) * P], w_xp[:, half, :],
                                                           start=(half == 0), stop=(half == HALVES - 1))
                            ins.then_inc(misc_full, 1)
                        elif step == "outproj" and tail(k):
                            pe.wait_ge(yg_ready, k)
                            claim(k, step)
                            for half in range(HALVES):
                                ins = nc.tensor.matmul(ps_m[:], w_out[:, half, :], yg[:, half, :],
                                                       start=(half == 0), stop=(half == HALVES - 1))
                            ins.then_inc(misc_full, 1)
                        elif step == "outT" and tail(k):
                            claim(k, step)
                            to_rows(oT, P, ident, ps_m).then_inc(misc_full, 1)

            iterations(pe, body)


_INS = ["x", "W_in", "b_in", "conv_w", "conv_b", "W_xp", "b_xp", "W_dt", "b_dt", "A_log", "D_skip", "W_out", "b_out",
        "alpha", "beta"]
_FFN = ["Wg", "W1", "W2", "W3", "Ws1", "Ws2", "Ws3"]


def kernel(**inputs):
    import concourse.bacc as bacc
    from concourse.bass_utils import run_bass_kernel_spmd

    nc = bacc.Bacc("TRN2", target_bir_lowering=False, num_devices=1)
    arrays, args = {}, []
    for name in [f"L0_attn_{n}" for n in _INS] + [f"L0_ffn_{n}" for n in _FFN]:
        a = np.ascontiguousarray(inputs[name])
        arrays[name] = a
        args.append(nc.dram_tensor(name, a.shape, mybir.dt.from_np(a.dtype), kind="ExternalInput").ap())
    shape = arrays["L0_attn_x"].shape
    out = nc.dram_tensor("out", shape, mybir.dt.float32, kind="ExternalOutput").ap()
    macaron_kernel(nc, *args, out)
    r = run_bass_kernel_spmd(nc, [arrays], core_ids=[0])
    return r.results[0]["out"]
```

```python
import math
from contextlib import ExitStack

import numpy as np
import concourse.bass as bass
from concourse import mybir


def macaron_kernel(nc, x, W_in, b_in, conv_w, conv_b, W_xp, b_xp, W_dt, b_dt, A_log, D_skip, W_out, b_out,
                   alpha, beta, Wg, W1, W2, W3, Ws1, Ws2, Ws3, out):
    F32, BF16, U32 = mybir.dt.float32, mybir.dt.bfloat16, mybir.dt.uint32
    ALU, ACT = mybir.AluOpType, mybir.ActivationFunctionType

    BATCH, LEN, C = x.shape
    E, _, H = W1.shape
    HS = Ws1.shape[1]
    DI = W_in.shape[1] // 2
    NS = A_log.shape[1]
    TAPS = conv_w.shape[2]
    P = 128
    NSEQ = 2
    TG = NSEQ * LEN
    TILES = TG // P
    G = BATCH // NSEQ
    HALVES = DI // P
    EH = E * H
    NCHUNK = -(-(EH + HS) // P)
    ECHUNK = EH // P
    LAST = EH + HS - (NCHUNK - 1) * P
    SLOTS = 2 * NS
    DI_TG = HALVES * TG
    PAD = TAPS - 1
    LN_EPS, STD_EPS = 1e-5, 1e-6
    PARTS = 3
    KP = 32 * PARTS
    ORDER = list(range(ECHUNK, NCHUNK)) + list(range(ECHUNK))

    def rows(j):
        return LAST if j == NCHUNK - 1 else P

    PLAN = {
        1: ["gate_y"], 2: ["outproj"], 3: ["x1n", "outT"], 4: ["resid"], 5: ["stats3"], 6: ["stats0"],
        7: ["ln_norm"], 8: ["norm0"], 11: ["stats1"], 12: ["norm1"], 13: ["xT1"], 14: ["xT0", "logits1"],
        15: ["route1"], 16: ["yT0", "addy0"], 17: ["stats2", "weights1"], 18: ["norm2", "wT1", "logits0"],
        19: ["route0", "xT2"], 20: ["in0"], 21: ["in1", "conv0a"], 22: ["in2", "conv0b", "conv1a"],
        23: ["in3", "conv1b"], 24: ["dt0", "weights0"], 25: ["dt1"], 26: ["xproj", "bcparts"],
        28: ["delta", "bcT"], 29: ["wT0"], 31: ["yT1", "addy1"],
    }
    UP0, UP1 = 0, 15
    DECAYS = {0: 2, 4: 4, 8: 6, 12: 8, 16: 10, 20: 12, 22: 14}
    MISC_ENTRY = ["xT0", "logits0", "wT0"]
    MISC_LEAD = ["yT0", "xT2", "in0", "in1", "in2", "in3", "dt0", "dt1", "xproj", "bcT"]
    MISC_TAIL = ["outproj", "outT", "xT1", "logits1", "wT1", "yT1"]

    def enters(k):
        return not isinstance(k, int) or 0 <= k + 2 < G

    def lead(k):
        return not isinstance(k, int) or 0 <= k + 1 < G

    def scans(k):
        return not isinstance(k, int) or 0 <= k < G

    def tail(k):
        return not isinstance(k, int) or k >= 1

    def misc_list(k):
        names = (enters(k) * MISC_ENTRY) + (lead(k) * MISC_LEAD) + (tail(k) * MISC_TAIL)
        return [n for s in range(SLOTS) for n in PLAN.get(s, []) if n in names]

    def before(k, names_of):
        if isinstance(k, int):
            return sum(len(names_of(i)) for i in range(-2, k))
        return sum(len(names_of(i)) for i in range(-2, 1)) + (k - 1) * len(names_of(1))

    def turn(k, name):
        return before(k, misc_list) + misc_list(k).index(name) + 1

    def turn_last(k, name):
        after = misc_list(k - 1 if isinstance(k, int) else 0)
        return before(k, misc_list) - (len(after) - 1 - after.index(name))

    def ffn_no(k, f):
        if isinstance(k, int) and k < 1:
            return k + 1
        if isinstance(k, int) and k >= G - 1:
            return 2 * (G - 1) + (k - (G - 1))
        return 2 * k + f

    def route_no(k, step):
        return ffn_no(k, 1) if step.endswith("1") else ffn_no(k + 1, 0)

    def fcount(k, f, per, n):
        return ffn_no(k, f) * per + n

    def f_parity(k, f):
        return ffn_no(k, f) % 2 if isinstance(k, int) else f

    def up_unit(k, slot):
        if UP0 <= slot < UP0 + NCHUNK and lead(k):
            return 0, slot - UP0
        if UP1 <= slot < UP1 + NCHUNK and tail(k):
            return 1, slot - UP1
        return None

    def gate_unit(k, slot):
        return up_unit(k, slot - 1) if slot else None

    def back_unit(k, slot):
        return up_unit(k, slot - 2) if slot > 1 else None

    def iterations(engine, body):
        body(-2, 0)
        body(-1, 1)
        body(0, 0)
        with engine.Fori(1, G - 3, 2) as k:
            body(k, 1)
            body(k + 1, 0)
        for k in range(G - 3, G + 1):
            body(k, k % 2)

    ctx = ExitStack()
    with ctx:
        def sb(name, shape, dt=F32):
            return ctx.enter_context(nc.sbuf_tensor(name, shape, dt))

        def pb(name, shape=(P, TG)):
            return ctx.enter_context(nc.psum_tensor(name, list(shape), F32))

        def sem(name):
            return ctx.enter_context(nc.semaphore(name))

        XS = 4
        xres = sb("xres", [P, XS, TILES, C])
        up_w = sb("up_w", [P, 2, EH + HS])
        down_w = sb("down_w", [P, NCHUNK, C])
        wg = sb("wg", [P, E])
        w_in = sb("w_in", [P, 2 * DI])
        w_dt = sb("w_dt", [P, HALVES, DI])
        w_xp = sb("w_xp", [P, HALVES, 2 * NS])
        w_out = sb("w_out", [P, HALVES, C])
        b_in_c = sb("b_in_c", [P, 2 * HALVES])
        conv_w_c = sb("conv_w_c", [P, HALVES, TAPS])
        conv_b_c = sb("conv_b_c", [P, HALVES])
        b_dt_c = sb("b_dt_c", [P, HALVES])
        d_c = sb("d_c", [P, HALVES])
        b_out_c = sb("b_out_c", [P, 1])
        a_log = sb("a_log", [P, HALVES, NS])
        a_exp = sb("a_exp", [P, HALVES, NS])
        a_neg = sb("a_neg", [P, HALVES, NS])
        b_xp_b = sb("b_xp_b", [P, 2 * NS])
        alpha_b = sb("alpha_b", [P, C])
        beta_b = sb("beta_b", [P, C])
        ident = sb("ident", [P, P])
        ident_bf = sb("ident_bf", [P, P], BF16)
        sel_bc = sb("sel_bc", [KP, 2 * NS, P], BF16)
        sel_w = sb("sel_w", [KP, ECHUNK, P], BF16)
        pow_mhalf = sb("pow_mhalf", [P, TILES])
        pow_half = sb("pow_half", [P, TILES])
        euler = sb("euler", [P, TILES])
        lanes = sb("lanes", [P, TILES * 2, E])
        carrier = sb("carrier", [P, 1])
        bnst = sb("bnst", [P, 4, TILES, 6])
        mv = [sb(f"mv{f}", [P, TILES, 2]) for f in range(2)]
        mv1 = sb("mvx", [P, 2, TILES, 2])
        rstd1 = sb("rstdx", [P, 2, TILES])
        mvr = sb("mvr", [P, TILES, 2])
        varp = sb("varp", [P, 4, TILES])
        rstd = [sb(f"rstd{f}", [P, TILES]) for f in range(2)]
        stdr = sb("stdr", [P, 3, TILES])
        xn = [sb(f"xn{f}", [P, TILES, C]) for f in range(3)]
        xnT = [sb(f"xnT{f}", [P, TG]) for f in range(3)]
        logit = sb("logit", [P, TILES, E])
        top = sb("top", [P, TILES, 8])
        topi = sb("topi", [P, TILES, 8], U32)
        topf = sb("topf", [P, TILES, 2])
        drop = sb("drop", [P, TILES])
        edrop = sb("edrop", [P, TILES])
        den = sb("den", [P, TILES])
        prob = sb("prob", [P, TILES, 2])
        hot = sb("hot", [P, TILES, 2, E])
        hotp = sb("hotp", [P, TILES, 2, E])
        wtok = sb("wtok", [P, TILES, E])
        wrem = sb("wrem", [P, TILES, E])
        wrem2 = sb("wrem2", [P, TILES, E])
        wparts = sb("wparts", [P, TILES, KP], BF16)
        wT = [sb(f"wT{f}", [KP, TG], BF16) for f in range(2)]
        NSILU = 4
        silu = sb("silu", [P, NSILU, TG])
        mid = sb("mid", [P, 2, TG])
        gated = sb("gated", [P, NSILU, TG])
        yT = [sb(f"yT{f}", [P, TG]) for f in range(2)]
        xin = sb("xin", [P, HALVES, NSEQ, PAD + LEN])
        conv = sb("conv", [P, HALVES, NSEQ, LEN])
        xconv = [sb(f"xconv{i}", [P, HALVES, TG]) for i in range(2)]
        zs = [sb(f"zs{i}", [P, HALVES, TG]) for i in range(2)]
        dpre = sb("dpre", [P, HALVES, TG])
        dtmp = sb("dtmp", [P, HALVES, TG])
        delta = [sb(f"delta{i}", [P, HALVES, TG]) for i in range(2)]
        du = [sb(f"du{i}", [P, HALVES, TG]) for i in range(2)]
        bc = sb("bc", [P, TILES, 2 * NS])
        bcrem = sb("bcrem", [P, TILES, 2 * NS])
        bcrem2 = sb("bcrem2", [P, TILES, 2 * NS])
        bcparts = sb("bcparts", [P, TILES, KP], BF16)
        bcT = [sb(f"bcT{i}", [KP, TG], BF16) for i in range(2)]
        NA, NC = 4, 4
        decay = sb("decay", [P, NA, HALVES, NSEQ, LEN])
        dbx = sb("dbx", [P, 2, HALVES, TG])
        hist = sb("hist", [P, 2, HALVES, TG])
        crow = sb("crow", [P, NC, TG])
        prod = sb("prod", [P, 2, HALVES, TG])
        yacc = [sb(f"yacc{i}", [P, HALVES, TG]) for i in range(2)]
        yg = sb("yg", [P, HALVES, TG])
        oT = sb("oT", [P, TG])
        rtok = sb("rtok", [P, TILES, C])
        ps_h1 = [pb("ps_h1a"), pb("ps_h1b")]
        ps_h2 = [pb("ps_h2a"), pb("ps_h2b")]
        ps_wb, ps_y, ps_bc, ps_m = (pb(n) for n in ("ps_wb", "ps_y", "ps_bc", "ps_m"))

        consts_loaded = sem("consts_loaded")
        consts_made = sem("consts_made")
        a_exped = sem("a_exped")
        a_ready = sem("a_ready")
        pads_zero = sem("pads_zero")
        x_loaded = sem("x_loaded")
        x_stored = sem("x_stored")
        misc_full = sem("misc_full")
        misc_taken = sem("misc_taken")
        var_ready = [sem(f"var_ready{i}") for i in range(4)]
        rstd_ready = [sem(f"rstd_ready{i}") for i in range(4)]
        norm_ready = [sem(f"norm_ready{i}") for i in range(3)]
        drop_ready = sem("drop_ready")
        edrop_ready = sem("edrop_ready")
        wparts_ready = sem("wparts_ready")
        h1_full, h2_full, wb_full = sem("h1_full"), sem("h2_full"), sem("wb_full")
        silu_done, mid_done, gate_done, down_done = sem("silu_done"), sem("mid_done"), sem("gate_done"), sem("down_done")
        y_taken = sem("y_taken")
        xin_ready, conv_ready, xconv_ready = sem("xin_ready"), sem("conv_ready"), sem("xconv_ready")
        zs_ready, logterm_ready, softplus_chain = sem("zs_ready"), sem("logterm_ready"), sem("softplus_chain")
        delta_ready, du_ready, bcparts_ready = sem("delta_ready"), sem("du_ready"), sem("bcparts_ready")
        decay_ready, b_full, c_full, crow_ready = sem("decay_ready"), sem("b_full"), sem("c_full"), sem("crow_ready")
        dbx_done, scan_done, prod_done, acc_done = sem("dbx_done"), sem("scan_done"), sem("prod_done"), sem("acc_done")
        yg_ready = sem("yg_ready")
        ln_ready, ln_scaled, ln_shifted = sem("ln_ready"), sem("ln_scaled"), sem("ln_shifted")
        mamba_added = sem("mamba_added")
        dve_stats, dve_route, dve_conv, dve_bc, dve_fin = (sem(n) for n in (
            "dve_stats", "dve_route", "dve_conv", "dve_bc", "dve_fin"))

        class Chain:

            def __init__(self, engine, sem, per, number):
                self.engine, self.sem, self.per, self.at, self.n = engine, sem, per, number * per, 0

            def link(self, ins):
                self.n += 1
                ins.then_inc(self.sem, 1)
                self.engine.wait_ge(self.sem, self.at + self.n)

            def end(self):
                assert self.n == self.per, (self.n, self.per)

        N_CONSTS, N_MADE = 22, 19
        ROUTE_LINKS, FIN_LINKS = 13, 4
        block = ctx.enter_context(nc.Block())

        @block.sync
        def _(sp):
            def load(g, slot):
                sp.dma_start(xres[:, slot, :, :],
                             x[bass.ds(g * NSEQ, NSEQ)].rearrange("b (t p) c -> p (b t) c", p=P)).then_inc(x_loaded, 16)

            def store(g, slot, k):
                sp.wait_ge(misc_taken, turn(k, "yT1"))
                sp.wait_ge(x_loaded, 16 * min(g + XS, G) if isinstance(k, int) else 16 * (g + XS))
                sp.dma_start(out[bass.ds(g * NSEQ, NSEQ)].rearrange("b (t p) c -> p (b t) c", p=P),
                             xres[:, slot, :, :]).then_inc(x_stored, 16)
                sp.wait_ge(x_stored, 16 * (g + 1))

            for g in range(XS):
                load(g, g)
                sp.wait_ge(x_loaded, 16 * (g + 1))
            with sp.Fori(1, G - XS + 1) as k:
                store(k - 1, (k - 1) % XS, k)
                load(k - 1 + XS, (k - 1) % XS)
            for k in range(G - XS + 1, G + 1):
                store(k - 1, (k - 1) % XS, k)

        @block.gpsimd
        def _(pool):
            made = 0

            def made_one(ins):
                nonlocal made
                made += 1
                ins.then_inc(consts_made, 1)
                pool.wait_ge(consts_made, made)

            made_one(nc.gpsimd.memset(ident[:], 0.0))
            made_one(nc.gpsimd.memset(ident_bf[:], 0.0))
            made_one(nc.gpsimd.memset(sel_bc[:], 0.0))
            made_one(nc.gpsimd.memset(sel_w[:], 1.0))
            made_one(nc.gpsimd.memset(pow_mhalf[:], -0.5))
            made_one(nc.gpsimd.memset(pow_half[:], 0.5))
            made_one(nc.gpsimd.memset(euler[:], math.e))
            made_one(nc.gpsimd.iota(lanes[:], [[0, TILES * 2], [1, E]], base=0, channel_multiplier=0,
                                    allow_small_or_imprecise_dtypes=True))
            for m in (ident, ident_bf):
                made_one(nc.gpsimd.affine_select(out=m[:], in_=m[:], compare_op=ALU.not_equal, fill=1.0, base=0,
                                                 pattern=[[-1, P]], channel_multiplier=1))
            for q in range(PARTS):
                part = sel_bc[32 * q:32 * q + 32, :, :]
                made_one(nc.gpsimd.affine_select(out=part, in_=part, compare_op=ALU.not_equal, fill=1.0, base=0,
                                                 pattern=[[-1, 2 * NS], [0, P]], channel_multiplier=1))
                part = sel_w[32 * q:32 * q + 32, :, :]
                made_one(nc.gpsimd.affine_select(out=part, in_=part, compare_op=ALU.is_ge, fill=0.0, base=0,
                                                 pattern=[[P, ECHUNK], [1, P]], channel_multiplier=-H))
            for q in range(PARTS):
                part = sel_w[32 * q:32 * q + 32, :, :]
                made_one(nc.gpsimd.affine_select(out=part, in_=part, compare_op=ALU.is_ge, fill=0.0, base=H - 1,
                                                 pattern=[[-P, ECHUNK], [-1, P]], channel_multiplier=H))

            def power(dst, src, exponent, ready, done, value):
                pool.wait_ge(ready, value)
                nc.gpsimd.tensor_tensor(dst, src, exponent, ALU.pow).then_inc(done, 1)

            def body(k, odd):
                nxt = 1 - odd
                behind = (k - 1) % XS if tail(k) else 0
                for slot in range(SLOTS):
                    for step in PLAN.get(slot, []):
                        if step == "stats0" and enters(k):
                            power(rstd[0][:], varp[:, 0, :], pow_mhalf[:], var_ready[0], rstd_ready[0], k + 3)
                        elif step == "stats1" and tail(k):
                            power(rstd[1][:], varp[:, 1, :], pow_mhalf[:], var_ready[1], rstd_ready[1], k)
                        elif step == "stats2" and lead(k):
                            power(rstd1[:, 1 - odd, :], varp[:, 2, :], pow_mhalf[:], var_ready[2],
                                  rstd_ready[2], k + 2)
                        elif step == "stats3" and tail(k):
                            power(stdr[:, 0, :], varp[:, 3, :], pow_half[:], var_ready[3], rstd_ready[3], k)
                        elif (step == "route0" and enters(k)) or (step == "route1" and tail(k)):
                            n = route_no(k, step) + 1
                            pool.wait_ge(drop_ready, n)
                            nc.gpsimd.tensor_tensor(edrop[:], euler[:], drop[:], ALU.pow).then_inc(edrop_ready, 1)
                        elif step == "ln_norm" and tail(k):
                            pool.wait_ge(ln_ready, k)
                            nc.gpsimd.tensor_tensor(rtok[:], rtok[:], alpha_b[:].unsqueeze(1).to_broadcast(
                                [P, TILES, C]), ALU.mult).then_inc(ln_scaled, 1)
                            pool.wait_ge(ln_scaled, k)
                            nc.gpsimd.tensor_tensor(rtok[:], rtok[:], beta_b[:].unsqueeze(1).to_broadcast(
                                [P, TILES, C]), ALU.add).then_inc(ln_shifted, 1)
                            pool.wait_ge(ln_shifted, k)
                            nc.gpsimd.tensor_tensor(xres[:, behind, :, :], xres[:, behind, :, :], rtok[:], ALU.add
                                                    ).then_inc(mamba_added, 1)
                    if scans(k) and slot % 2 == 0:
                        s = slot // 2
                        c_all = crow[:, s % NC, :].unsqueeze(1).to_broadcast([P, HALVES, TG])
                        pool.wait_ge(scan_done, NS * k + s + 1)
                        pool.wait_ge(crow_ready, NS * k + s + 1)
                        if s == 0:
                            nc.gpsimd.tensor_tensor(yacc[odd][:], hist[:, s % 2, :, :], c_all, ALU.mult
                                                    ).then_inc(prod_done, 1)
                        else:
                            if s > 2 or not isinstance(k, int) or k > 0:
                                pool.wait_ge(acc_done, (NS - 1) * k + s - 2 + (s == 1))
                            nc.gpsimd.tensor_tensor(prod[:, s % 2, :, :], hist[:, s % 2, :, :], c_all, ALU.mult
                                                    ).then_inc(prod_done, 1)
                        if s > 1:
                            accumulate(k, odd, s - 1)
                        if s == NS - 1:
                            accumulate(k, odd, s)

            def accumulate(k, odd, s):
                pool.wait_ge(prod_done, NS * k + s + 1)
                if s > 1:
                    pool.wait_ge(acc_done, (NS - 1) * k + s - 1)
                nc.gpsimd.tensor_tensor(yacc[odd][:], yacc[odd][:], prod[:, s % 2, :, :], ALU.add
                                        ).then_inc(acc_done, 1)

            iterations(pool, body)

        @block.scalar
        def _(act):
            n_const = 0

            def const(dst, src):
                nonlocal n_const
                n_const += 1
                act.dma_start(dst, src).then_inc(consts_loaded, 16)

            with nc.allow_non_contiguous_dma(reason="small constants in column form"):
                const(a_log[:], A_log.rearrange("(h p) s -> p h s", p=P))
                const(wg[:], Wg[:, :])
                for i, (we, ws) in enumerate(((W1, Ws1), (W2, Ws2))):
                    const(up_w[:, i, 0:EH].rearrange("c (e h) -> c e h", e=E), we.rearrange("e c h -> c e h"))
                    const(up_w[:, i, EH:EH + HS], ws[:, :])
                const(down_w[:, 0:ECHUNK, :], W3.rearrange("e h c -> (e h) c").rearrange("(j p) c -> p j c", p=P))
                full = HS // P
                const(down_w[:, ECHUNK:ECHUNK + full, :], Ws3[0:full * P, :].rearrange("(j p) c -> p j c", p=P))
                const(down_w[0:LAST, NCHUNK - 1, :], Ws3[full * P:HS, :])
                const(w_in[:], W_in[:, :])
                const(w_dt[:], W_dt.rearrange("(h p) n -> p h n", p=P))
                const(w_xp[:], W_xp.rearrange("(h p) n -> p h n", p=P))
                const(w_out[:], W_out.rearrange("(h p) n -> p h n", p=P))
                const(b_in_c[:], b_in.rearrange("(h p) -> p h", p=P))
                const(conv_w_c[:], conv_w.rearrange("(h p) o t -> p h (o t)", p=P))
                const(conv_b_c[:], conv_b.rearrange("(h p) -> p h", p=P))
                const(b_dt_c[:], b_dt.rearrange("(h p) -> p h", p=P))
                const(d_c[:], D_skip.rearrange("(h p) -> p h", p=P))
                const(b_out_c[:], b_out.rearrange("(h p) -> p h", p=P))
                const(b_xp_b[:], b_xp.partition_broadcast(P))
                const(alpha_b[:], alpha.partition_broadcast(P))
                const(beta_b[:], beta.partition_broadcast(P))
            assert n_const == N_CONSTS, n_const
            act.wait_ge(consts_loaded, 16 * n_const)
            nc.scalar.activation(a_exp[:], a_log[:], ACT.Exp).then_inc(a_exped, 1)
            act.wait_ge(a_ready, 1)
            act.wait_ge(pads_zero, 5)

            def take(k, name):
                act.wait_ge(misc_full, turn(k, name))

            def decays(g, par, states):
                for s in states:
                    if s >= NA or not isinstance(g, int) or g > 0:
                        act.wait_ge(scan_done, NS * g + s - NA + 1)
                    if s == 0:
                        act.wait_ge(delta_ready, g + 1)
                    for half in range(HALVES):
                        d = delta[par][:, half, :].rearrange("p (b t) -> p b t", b=NSEQ)
                        ins = nc.scalar.activation(decay[:, s % NA, half, :, 1:LEN], d[:, :, 1:LEN], ACT.Exp,
                                                   scale=a_neg[:, half, s:s + 1])
                    ins.then_inc(decay_ready, 1)

            def copy_c(g, s):
                act.wait_ge(c_full, NS * g + s + 1)
                if s >= NC or not isinstance(g, int) or g > 0:
                    act.wait_ge(prod_done, NS * g + s - NC + 1)
                nc.scalar.activation(crow[:, s % NC, :], ps_bc[:], ACT.Copy).then_inc(crow_ready, 1)

            def body(k, odd):
                nxt = 1 - odd
                for slot in range(SLOTS):
                    if slot == SLOTS - 2 and lead(k):
                        copy_c(k + 1, 0)
                    elif slot % 2 == 0 and scans(k) and slot < SLOTS - 2:
                        copy_c(k, slot // 2 + 1)
                    if "dt1" in PLAN.get(slot - 1, []) and lead(k):
                        act.wait_ge(softplus_chain, (HALVES + 1) * (k + 2))
                        nc.scalar.activation(dtmp[:], dtmp[:], ACT.Ln, bias=1.0).then_inc(logterm_ready, 1)
                    u = up_unit(k, slot)
                    if u is not None:
                        f, pos = u
                        r = rows(ORDER[pos])
                        n = fcount(k, f, NCHUNK, pos)
                        act.wait_ge(h1_full, n + 1)
                        if not isinstance(n, int) or n >= NSILU:
                            act.wait_ge(gate_done, n - NSILU + 1)
                        place = (pos + NCHUNK * f_parity(k, f)) % NSILU
                        nc.scalar.activation(silu[0:r, place, :], ps_h1[pos % 2][0:r, :],
                                             ACT.Silu).then_inc(silu_done, 1)
                    for step in PLAN.get(slot, []):
                        if step == "xT0" and enters(k) or step == "xT1" and tail(k) or step == "xT2" and lead(k):
                            take(k, step)
                            nc.scalar.activation(xnT[int(step[2])][:], ps_m[:], ACT.Copy).then_inc(misc_taken, 1)
                        elif step == "wT0" and enters(k) or step == "wT1" and tail(k):
                            take(k, step)
                            nc.scalar.activation(wT[int(step[2])][:], ps_m[0:KP, 0:TG // 2].bitcast(BF16),
                                                 ACT.Copy).then_inc(misc_taken, 1)
                        elif step == "bcT" and lead(k):
                            take(k, step)
                            nc.scalar.activation(bcT[nxt][:], ps_m[0:KP, 0:TG // 2].bitcast(BF16),
                                                 ACT.Copy).then_inc(misc_taken, 1)
                        elif step == "yT0" and lead(k) or step == "yT1" and tail(k):
                            f = int(step[2])
                            act.wait_ge(down_done, fcount(k, f, NCHUNK, NCHUNK))
                            nc.scalar.activation(yT[f][:], ps_y[:], ACT.Copy).then_inc(y_taken, 1)
                        elif step == "outproj" and tail(k):
                            take(k, step)
                            nc.scalar.activation(oT[:], ps_m[:], ACT.Identity,
                                                 bias=b_out_c[:, 0:1]).then_inc(misc_taken, 1)
                        elif step in ("in0", "in1") and lead(k):
                            half = int(step[2])
                            take(k, step)
                            nc.scalar.activation(xin[:, half, :, PAD:PAD + LEN],
                                                 ps_m[:].rearrange("p (b t) -> p b t", b=NSEQ), ACT.Identity,
                                                 bias=b_in_c[:, half:half + 1]).then_inc(misc_taken, 1)
                        elif step in ("in2", "in3") and lead(k):
                            half = int(step[2]) - HALVES
                            take(k, step)
                            nc.scalar.activation(zs[nxt][:, half, :], ps_m[:], ACT.Silu,
                                                 bias=b_in_c[:, HALVES + half:HALVES + half + 1]
                                                 ).then_inc(misc_taken, 1)
                        elif step in ("conv0b", "conv1b") and lead(k):
                            half = int(step[4])
                            act.wait_ge(conv_ready, HALVES * (k + 1) + half + 1)
                            nc.scalar.activation(xconv[nxt][:, half, :],
                                                 conv[:, half, :, :].rearrange("p b t -> p (b t)"), ACT.Silu,
                                                 bias=conv_b_c[:, half:half + 1]).then_inc(xconv_ready, 1)
                        elif step in ("dt0", "dt1") and lead(k):
                            half = int(step[2])
                            take(k, step)
                            nc.scalar.activation(dtmp[:, half, :], ps_m[:], ACT.Abs,
                                                 bias=b_dt_c[:, half:half + 1]).then_inc(softplus_chain, 1)
                            nc.scalar.activation(dpre[:, half, :], ps_m[:], ACT.Identity,
                                                 bias=b_dt_c[:, half:half + 1]).then_inc(misc_taken, 1)
                            if half == HALVES - 1:
                                act.wait_ge(softplus_chain, (HALVES + 1) * (k + 2) - 1)
                                nc.scalar.activation(dtmp[:], dtmp[:], ACT.Exp, scale=-1.0
                                                     ).then_inc(softplus_chain, 1)
                    if slot == SLOTS - 1 and lead(k):
                        decays(k + 1, nxt, range(NA // 2))
                    elif slot in DECAYS and scans(k):
                        decays(k, odd, range(DECAYS[slot], DECAYS[slot] + 2))

            iterations(act, body)

        @block.vector
        def _(dve):
            nc.vector.memset(xin[:, :, :, 0:PAD], 0.0).then_inc(pads_zero, 1)
            nc.vector.memset(decay[:, :, :, :, 0:1], 0.0).then_inc(pads_zero, 1)
            nc.vector.memset(wparts[:], 0.0).then_inc(pads_zero, 1)
            nc.vector.memset(bcparts[:], 0.0).then_inc(pads_zero, 1)
            dve.wait_ge(a_exped, 1)
            nc.vector.tensor_scalar(a_neg[:], a_exp[:], -1.0, None, ALU.mult).then_inc(a_ready, 1)
            nc.vector.memset(mid[:], 0.0).then_inc(pads_zero, 1)
            dve.wait_ge(consts_loaded, 16 * N_CONSTS)
            dve.wait_ge(consts_made, N_MADE)
            dve.wait_ge(pads_zero, 5)

            def plain_wait():
                dve.wait_ge(pads_zero, 5)

            def statistics(src, which, agg, number, scale, shift):
                chain = Chain(dve, dve_stats, 2, number)
                for t in range(TILES):
                    ins = nc.vector.bn_stats(bnst[:, which, t, :], src[:, t, :])
                chain.link(ins)
                nc.vector.memset(carrier[:], 0.0)
                for t in range(TILES):
                    ins = nc.vector.bn_aggr(agg[:, t, :], bnst[:, which, t, :])
                chain.link(ins)
                chain.end()
                nc.vector.tensor_scalar(varp[:, which, :], agg[:, :, 1], scale, shift, ALU.mult, ALU.add
                                        ).then_inc(var_ready[which], 1)

            STATS = {"stats0": 0, "stats1": 1, "stats2": 2, "stats3": 3}

            def stats_list(k):
                there = {"stats0": enters(k), "stats1": tail(k), "stats2": lead(k), "stats3": tail(k)}
                return [STATS[n] for s in range(SLOTS) for n in PLAN.get(s, []) if there.get(n)]

            def stats_no(k, which):
                return before(k, stats_list) + stats_list(k).index(which)

            def normalise(dst, src, agg, inv):
                for t in range(TILES):
                    ins = nc.vector.tensor_scalar(dst[:, t, :], src[:, t, :], agg[:, t, 0:1], inv[:, t:t + 1],
                                                  ALU.subtract, ALU.mult)
                return ins

            def split(chain, whole, rem, rem2, parts, width):
                hi, md, lo = (parts[:, :, 32 * q:32 * q + width] for q in range(PARTS))
                chain.link(nc.vector.tensor_copy(hi, whole))
                chain.link(nc.vector.tensor_tensor(rem, whole, hi, ALU.subtract))
                chain.link(nc.vector.tensor_copy(md, rem))
                chain.link(nc.vector.tensor_tensor(rem2, rem, md, ALU.subtract))
                return nc.vector.tensor_copy(lo, rem2)

            route_chain = fin_chain = conv_chain = conv_last = None

            def input_term(g, par, s):
                dve.wait_ge(b_full, NS * g + s + 1)
                if s == 0:
                    dve.wait_ge(du_ready, g + 1)
                nc.vector.tensor_tensor(dbx[:, s % 2, :, :], du[par][:],
                                        ps_bc[:].unsqueeze(1).to_broadcast([P, HALVES, TG]), ALU.mult
                                        ).then_inc(dbx_done, 1)

            def body(k, odd):
                nonlocal route_chain, fin_chain, conv_chain, conv_last
                nxt = 1 - odd
                entering, ahead, behind = (k + 2) % XS, (k + 1) % XS, (k - 1) % XS if tail(k) else 0
                for slot in range(SLOTS):
                    d = gate_unit(k, slot)
                    if d is not None:
                        f, pos = d
                        j = ORDER[pos]
                        r = rows(j)
                        n = fcount(k, f, NCHUNK, pos)
                        place = (pos + NCHUNK * f_parity(k, f)) % NSILU
                        dve.wait_ge(silu_done, n + 1)
                        dve.wait_ge(h2_full, n + 1)
                        if j >= ECHUNK:
                            if not isinstance(n, int) or n >= NSILU:
                                dve.wait_ge(down_done, n - NSILU + 1)
                            nc.vector.tensor_tensor(gated[0:r, place, :], silu[0:r, place, :], ps_h2[pos % 2][0:r, :],
                                                    ALU.mult).then_inc(gate_done, 1)
                        else:
                            nc.vector.tensor_tensor(mid[:, pos % 2, :], silu[:, place, :], ps_h2[pos % 2][:], ALU.mult
                                                    ).then_inc(mid_done, 1)
                    if slot == SLOTS - 1:
                        if lead(k):
                            input_term(k + 1, nxt, 0)
                    elif scans(k) and slot % 2:
                        input_term(k, odd, slot // 2 + 1)
                    if scans(k) and slot % 2 == 0:
                        s = slot // 2
                        dve.wait_ge(dbx_done, NS * k + s + 1)
                        dve.wait_ge(decay_ready, NS * k + s + 1)
                        if s > 1 or not isinstance(k, int) or k > 0:
                            dve.wait_ge(prod_done, NS * k + s - 1)
                        nc.vector.tensor_tensor_scan(hist[:, s % 2, :, :].rearrange("p h t -> p (h t)"),
                                                     decay[:, s % NA, :, :, :].rearrange("p h b t -> p (h b t)"),
                                                     dbx[:, s % 2, :, :].rearrange("p h t -> p (h t)"), 0.0,
                                                     ALU.mult, ALU.add).then_inc(scan_done, 1)
                    if d is not None and j < ECHUNK:
                        dve.wait_ge(mid_done, fcount(k, f, ECHUNK, pos - (NCHUNK - ECHUNK) + 1))
                        dve.wait_ge(wb_full, fcount(k, f, ECHUNK, pos - (NCHUNK - ECHUNK) + 1))
                        if not isinstance(n, int) or n >= NSILU:
                            dve.wait_ge(down_done, n - NSILU + 1)
                        nc.vector.tensor_tensor(gated[:, place, :], mid[:, pos % 2, :], ps_wb[:], ALU.mult
                                                ).then_inc(gate_done, 1)
                    for step in PLAN.get(slot, []):
                        if step == "stats0" and enters(k):
                            plain_wait()
                            dve.wait_ge(x_loaded, 16 * (k + 3))
                            statistics(xres[:, entering, :, :], 0, mv[0], stats_no(k, 0), 1.0, LN_EPS)
                        elif step == "stats1" and tail(k):
                            plain_wait()
                            dve.wait_ge(mamba_added, k)
                            statistics(xres[:, behind, :, :], 1, mv[1], stats_no(k, 1), 1.0, LN_EPS)
                        elif step == "stats2" and lead(k):
                            plain_wait()
                            dve.wait_ge(misc_taken, turn(k, "yT0"))
                            statistics(xres[:, ahead, :, :], 2, mv1[:, nxt, :, :], stats_no(k, 2), 1.0, LN_EPS)
                        elif step == "norm0" and enters(k):
                            dve.wait_ge(rstd_ready[0], k + 3)
                            normalise(xn[0], xres[:, entering, :, :], mv[0], rstd[0]).then_inc(norm_ready[0], 1)
                        elif step == "norm1" and tail(k):
                            dve.wait_ge(rstd_ready[1], k)
                            normalise(xn[1], xres[:, behind, :, :], mv[1], rstd[1]).then_inc(norm_ready[1], 1)
                        elif step == "norm2" and lead(k):
                            dve.wait_ge(rstd_ready[2], k + 2)
                            normalise(xn[2], xres[:, ahead, :, :], mv1[:, nxt, :, :], rstd1[:, nxt, :]
                                      ).then_inc(norm_ready[2], 1)
                        elif step == "route0" and enters(k) or step == "route1" and tail(k):
                            f = int(step[5])
                            dve.wait_ge(misc_full, turn(k, f"logits{f}"))
                            nc.vector.tensor_copy(logit[:], ps_m[:, 0:TILES * E].rearrange("p (t e) -> p t e", e=E)
                                                  ).then_inc(misc_taken, 1)
                            plain_wait()
                            dve.wait_ge(misc_taken, turn(k, f"logits{f}"))
                            chain = Chain(dve, dve_route, ROUTE_LINKS, route_no(k, step))
                            for t in range(TILES):
                                ins = nc.vector.max(top[:, t, :], logit[:, t, :])
                            chain.link(ins)
                            nc.vector.tensor_tensor(drop[:], top[:, :, 1], top[:, :, 0], ALU.subtract
                                                    ).then_inc(drop_ready, 1)
                            for t in range(TILES):
                                ins = nc.vector.max_index(topi[:, t, :], top[:, t, :], logit[:, t, :])
                            chain.link(ins)
                            chain.link(nc.vector.tensor_copy(topf[:], topi[:, :, 0:2]))
                            chain.link(nc.vector.tensor_tensor(
                                hot[:].rearrange("p t i e -> p (t i) e"), lanes[:],
                                topf[:].rearrange("p t i -> p (t i)").unsqueeze(2).to_broadcast([P, TILES * 2, E]),
                                ALU.is_equal))
                            route_chain = chain
                        elif step == "weights0" and enters(k) or step == "weights1" and tail(k):
                            f = int(step[7])
                            chain = route_chain
                            dve.wait_ge(edrop_ready, route_no(k, step) + 1)
                            chain.link(nc.vector.tensor_scalar(den[:], edrop[:], 1.0, None, ALU.add))
                            chain.link(nc.vector.reciprocal(prob[:, :, 0], den[:]))
                            chain.link(nc.vector.tensor_tensor(prob[:, :, 1], edrop[:], prob[:, :, 0], ALU.mult))
                            chain.link(nc.vector.tensor_tensor(
                                hotp[:].rearrange("p t i e -> p (t i) e"), hot[:].rearrange("p t i e -> p (t i) e"),
                                prob[:].rearrange("p t i -> p (t i)").unsqueeze(2).to_broadcast([P, TILES * 2, E]),
                                ALU.mult))
                            chain.link(nc.vector.tensor_tensor(wtok[:], hotp[:, :, 0, :], hotp[:, :, 1, :], ALU.add))
                            split(chain, wtok[:], wrem[:], wrem2[:], wparts, E).then_inc(wparts_ready, 1)
                            chain.end()
                        elif step == "yT0" and lead(k) or step == "yT1" and tail(k):
                            pass
                        elif step == "addy0" and lead(k) or step == "addy1" and tail(k):
                            f = int(step[4])
                            dve.wait_ge(misc_full, turn(k, f"yT{f}"))
                            xr = xres[:, behind if f else ahead, :, :].rearrange("p t c -> p (t c)")
                            nc.vector.scalar_tensor_tensor(xr, ps_m[:], 0.5, xr, ALU.mult, ALU.add
                                                           ).then_inc(misc_taken, 1)
                        elif step in ("conv0a", "conv1a") and lead(k):
                            half = int(step[4])
                            acc = conv[:, half, :, :]
                            dve.wait_ge(misc_taken, turn(k, f"in{half}"))
                            conv_chain = Chain(dve, dve_conv, TAPS - 1, HALVES * (k + 1) + half)
                            conv_chain.link(nc.vector.tensor_scalar(acc, xin[:, half, :, 0:LEN],
                                                                    conv_w_c[:, half, 0:1], None, ALU.mult))
                            conv_last = nc.vector.scalar_tensor_tensor(acc, xin[:, half, :, 1:1 + LEN],
                                                                       conv_w_c[:, half, 1:2], acc, ALU.mult, ALU.add)
                        elif step in ("conv0b", "conv1b") and lead(k):
                            half = int(step[4])
                            acc = conv[:, half, :, :]
                            for tap in range(2, TAPS):
                                conv_chain.link(conv_last)
                                conv_last = nc.vector.scalar_tensor_tensor(acc, xin[:, half, :, tap:tap + LEN],
                                                                           conv_w_c[:, half, tap:tap + 1], acc,
                                                                           ALU.mult, ALU.add)
                            conv_chain.end()
                            conv_last.then_inc(conv_ready, 1)
                        elif step == "delta" and lead(k):
                            dve.wait_ge(logterm_ready, k + 2)
                            nc.vector.scalar_tensor_tensor(delta[nxt][:], dpre[:], 0.0, dtmp[:], ALU.max, ALU.add
                                                           ).then_inc(delta_ready, 1)
                            dve.wait_ge(delta_ready, k + 2)
                            nc.vector.tensor_tensor(du[nxt][:], delta[nxt][:], xconv[nxt][:], ALU.mult
                                                    ).then_inc(du_ready, 1)
                        elif step == "bcparts" and lead(k):
                            dve.wait_ge(misc_full, turn(k, "xproj"))
                            nc.vector.tensor_tensor(
                                bc[:], ps_m[:, 0:TILES * 2 * NS].rearrange("p (t n) -> p t n", t=TILES),
                                b_xp_b[:].unsqueeze(1).to_broadcast([P, TILES, 2 * NS]), ALU.add
                            ).then_inc(misc_taken, 1)
                            dve.wait_ge(misc_taken, turn(k, "xproj"))
                            chain = Chain(dve, dve_bc, 4, k + 1)
                            split(chain, bc[:], bcrem[:], bcrem2[:], bcparts, 2 * NS).then_inc(bcparts_ready, 1)
                            chain.end()
                        elif step == "gate_y" and tail(k):
                            dve.wait_ge(acc_done, (NS - 1) * k)
                            chain = Chain(dve, dve_fin, FIN_LINKS, k - 1)
                            for half in range(HALVES):
                                ins = nc.vector.scalar_tensor_tensor(yg[:, half, :], xconv[nxt][:, half, :],
                                                                     d_c[:, half:half + 1], yacc[nxt][:, half, :],
                                                                     ALU.mult, ALU.add)
                            chain.link(ins)
                            nc.vector.tensor_tensor(yg[:], yg[:], zs[nxt][:], ALU.mult).then_inc(yg_ready, 1)
                            fin_chain = chain
                        elif step == "x1n" and tail(k):
                            fin_chain.link(normalise(rtok, xres[:, behind, :, :], mv1[:, nxt, :, :],
                                                     rstd1[:, nxt, :]))
                        elif step == "resid" and tail(k):
                            dve.wait_ge(misc_full, turn(k, "outT"))
                            r2 = rtok[:].rearrange("p t c -> p (t c)")
                            nc.vector.tensor_tensor(r2, r2, ps_m[:], ALU.add).then_inc(misc_taken, 1)
                        elif step == "stats3" and tail(k):
                            plain_wait()
                            dve.wait_ge(misc_taken, turn(k, "outT"))
                            statistics(rtok, 3, mvr, stats_no(k, 3), C / (C - 1), 0.0)
                        elif step == "ln_norm" and tail(k):
                            chain = fin_chain
                            dve.wait_ge(rstd_ready[3], k)
                            chain.link(nc.vector.tensor_scalar(stdr[:, 1, :], stdr[:, 0, :], STD_EPS, None, ALU.add))
                            chain.link(nc.vector.reciprocal(stdr[:, 2, :], stdr[:, 1, :]))
                            chain.end()
                            normalise(rtok, rtok, mvr, stdr[:, 2, :]).then_inc(ln_ready, 1)

            iterations(dve, body)

        @block.tensor
        def _(pe):
            pe.wait_ge(consts_loaded, 16 * N_CONSTS)
            pe.wait_ge(consts_made, N_MADE)

            def claim(k, name):
                n = turn(k, name) - 1
                if not isinstance(n, int) or n > 0:
                    pe.wait_ge(misc_taken, n)

            def to_rows(src, width, idn, dst):
                for t in range(TILES):
                    ins = nc.tensor.transpose(dst[0:width, t * P:(t + 1) * P], src[:, t, :] if len(src.shape) == 3
                                              else src[:, t * P:(t + 1) * P], idn[:])
                return ins

            def row_c(g, par, s):
                if s or not isinstance(g, int) or g > 0:
                    pe.wait_ge(dbx_done, NS * g + s)
                nc.tensor.matmul(ps_bc[:], sel_bc[:, NS + s, :], bcT[par][:], start=True, stop=True
                                 ).then_inc(c_full, 1)

            def row_b(g, par, s):
                pe.wait_ge(crow_ready, NS * g + s + 1)
                nc.tensor.matmul(ps_bc[:], sel_bc[:, s, :], bcT[par][:], start=True, stop=True).then_inc(b_full, 1)

            def body(k, odd):
                nxt = 1 - odd
                for slot in range(SLOTS):
                    if slot == SLOTS - 2 and lead(k):
                        pe.wait_ge(misc_taken, turn(k, "bcT"))
                        row_c(k + 1, nxt, 0)
                    elif slot == SLOTS - 1 and lead(k):
                        row_b(k + 1, nxt, 0)
                    elif scans(k) and slot < SLOTS - 2:
                        (row_b if slot % 2 else row_c)(k, odd, slot // 2 + 1)
                    g = gate_unit(k, slot)
                    if g is not None and ORDER[g[1]] < ECHUNK:
                        f, pos = g
                        if ORDER[pos] == 0:
                            pe.wait_ge(misc_taken, turn(k, "wT1") if f else turn_last(k, "wT0"))
                        pe.wait_ge(gate_done, fcount(k, f, NCHUNK, pos))
                        nc.tensor.matmul(ps_wb[:], sel_w[:, ORDER[pos], :], wT[f][:], start=True, stop=True
                                         ).then_inc(wb_full, 1)
                    u = up_unit(k, slot)
                    if u is not None:
                        f, pos = u
                        j = ORDER[pos]
                        r = rows(j)
                        n = fcount(k, f, NCHUNK, pos)
                        if pos == 0:
                            pe.wait_ge(misc_taken, turn(k, "xT1") if f else turn_last(k, "xT0"))
                        if not isinstance(n, int) or n >= 2:
                            pe.wait_ge(silu_done, n - 1)
                        nc.tensor.matmul(ps_h1[pos % 2][0:r, :], up_w[:, 0, j * P:j * P + r], xnT[f][:],
                                         start=True, stop=True).then_inc(h1_full, 1)
                    d = back_unit(k, slot)
                    if d is not None:
                        fd, posd = d
                        jd = ORDER[posd]
                        rd = rows(jd)
                        pe.wait_ge(gate_done, fcount(k, fd, NCHUNK, posd + 1))
                        if posd == 0 and (not isinstance(k, int) or k >= 0):
                            pe.wait_ge(y_taken, ffn_no(k, fd))
                        nc.tensor.matmul(ps_y[:], down_w[0:rd, jd, :], gated[0:rd, (posd + NCHUNK * f_parity(k, fd)) % NSILU, :], start=(posd == 0),
                                         stop=(posd == NCHUNK - 1)).then_inc(down_done, 1)
                    if u is not None:
                        if not isinstance(n, int) or n >= 2:
                            pe.wait_ge(gate_done, n - 1)
                        nc.tensor.matmul(ps_h2[pos % 2][0:r, :], up_w[:, 1, j * P:j * P + r], xnT[f][:],
                                         start=True, stop=True).then_inc(h2_full, 1)
                    for step in PLAN.get(slot, []):
                        if step == "xT0" and enters(k) or step == "xT1" and tail(k) or step == "xT2" and lead(k):
                            f = int(step[2])
                            pe.wait_ge(norm_ready[f], (k + 3, k, k + 2)[f])
                            claim(k, step)
                            to_rows(xn[f], P, ident, ps_m).then_inc(misc_full, 1)
                        elif step == "logits0" and enters(k) or step == "logits1" and tail(k):
                            f = int(step[6])
                            claim(k, step)
                            for t in range(TILES):
                                ins = nc.tensor.matmul(ps_m[:, t * E:(t + 1) * E], xnT[f][:, t * P:(t + 1) * P],
                                                       wg[:], start=True, stop=True)
                            ins.then_inc(misc_full, 1)
                        elif step == "wT0" and enters(k) or step == "wT1" and tail(k):
                            pe.wait_ge(wparts_ready, route_no(k, step) + 1)
                            claim(k, step)
                            to_rows(wparts, KP, ident_bf, ps_m[:, 0:TG // 2].bitcast(BF16)).then_inc(misc_full, 1)
                        elif step == "bcT" and lead(k):
                            pe.wait_ge(bcparts_ready, k + 2)
                            claim(k, step)
                            to_rows(bcparts, KP, ident_bf, ps_m[:, 0:TG // 2].bitcast(BF16)).then_inc(misc_full, 1)
                        elif step == "yT0" and lead(k) or step == "yT1" and tail(k):
                            f = int(step[2])
                            pe.wait_ge(y_taken, ffn_no(k, f) + 1)
                            claim(k, step)
                            to_rows(yT[f], P, ident, ps_m).then_inc(misc_full, 1)
                        elif step in ("in0", "in1", "in2", "in3") and lead(k):
                            c = int(step[2])
                            claim(k, step)
                            nc.tensor.matmul(ps_m[:], w_in[:, c * P:(c + 1) * P], xnT[2][:], start=True, stop=True
                                             ).then_inc(misc_full, 1)
                        elif step in ("dt0", "dt1") and lead(k):
                            c = int(step[2])
                            pe.wait_ge(xconv_ready, HALVES * (k + 2))
                            claim(k, step)
                            for half in range(HALVES):
                                ins = nc.tensor.matmul(ps_m[:], w_dt[:, half, c * P:(c + 1) * P],
                                                       xconv[nxt][:, half, :], start=(half == 0),
                                                       stop=(half == HALVES - 1))
                            ins.then_inc(misc_full, 1)
                        elif step == "xproj" and lead(k):
                            pe.wait_ge(xconv_ready, HALVES * (k + 2))
                            claim(k, step)
                            for t in range(TILES):
                                for half in range(HALVES):
                                    ins = nc.tensor.matmul(ps_m[:, t * 2 * NS:(t + 1) * 2 * NS],
                                                           xconv[nxt][:, half, t * P:(t + 1) * P], w_xp[:, half, :],
                                                           start=(half == 0), stop=(half == HALVES - 1))
                            ins.then_inc(misc_full, 1)
                        elif step == "outproj" and tail(k):
                            pe.wait_ge(yg_ready, k)
                            claim(k, step)
                            for half in range(HALVES):
                                ins = nc.tensor.matmul(ps_m[:], w_out[:, half, :], yg[:, half, :],
                                                       start=(half == 0), stop=(half == HALVES - 1))
                            ins.then_inc(misc_full, 1)
                        elif step == "outT" and tail(k):
                            claim(k, step)
                            to_rows(oT, P, ident, ps_m).then_inc(misc_full, 1)

            iterations(pe, body)


_INS = ["x", "W_in", "b_in", "conv_w", "conv_b", "W_xp", "b_xp", "W_dt", "b_dt", "A_log", "D_skip", "W_out", "b_out",
        "alpha", "beta"]
_FFN = ["Wg", "W1", "W2", "W3", "Ws1", "Ws2", "Ws3"]


def kernel(**inputs):
    import concourse.bacc as bacc
    from concourse.bass_utils import run_bass_kernel_spmd

    nc = bacc.Bacc("TRN2", target_bir_lowering=False, num_devices=1)
    arrays, args = {}, []
    for name in [f"L0_attn_{n}" for n in _INS] + [f"L0_ffn_{n}" for n in _FFN]:
        a = np.ascontiguousarray(inputs[name])
        arrays[name] = a
        args.append(nc.dram_tensor(name, a.shape, mybir.dt.from_np(a.dtype), kind="ExternalInput").ap())
    shape = arrays["L0_attn_x"].shape
    out = nc.dram_tensor("out", shape, mybir.dt.float32, kind="ExternalOutput").ap()
    macaron_kernel(nc, *args, out)
    r = run_bass_kernel_spmd(nc, [arrays], core_ids=[0])
    return r.results[0]["out"]
```
